# Optimizing a Trainium2 kernel written in Bass

```python
import numpy as np
import jax
import jax.numpy as jnp

def _softmax(x, axis=-1):
    return jax.nn.softmax(x, axis=axis)

def _gelu(x):
    return jax.nn.gelu(x, approximate=True)

def _silu(x):
    return jax.nn.silu(x)

def _sigmoid(x):
    return jax.nn.sigmoid(x)

def _layernorm(x, axis=-1, eps=1e-05):
    m = jnp.mean(x, axis=axis, keepdims=True)
    v = jnp.var(x, axis=axis, keepdims=True)
    return (x - m) / jnp.sqrt(v + eps)

def _scatter_add(tgt, idx, src, axis=0):
    return tgt.at[idx].add(src)

def _segment_sum(src, seg, n):
    return jax.ops.segment_sum(src, seg, n)
kernel_name = 'mk_decoder_postln_d1_seqx_r8_07e46f'

def setup_inputs(seed: int=0):
    np.random.seed(seed)
    _w = jnp.asarray

    def _rec_inputs():
        import jax
        import jax.numpy as jnp
        _rk = jax.random.key(seed)
        x = 7.22e-05 + 1 * jax.random.normal(jax.random.fold_in(_rk, 1), (4, 256, 256), jnp.float32)
        _lenS = 256 - jax.random.randint(jax.random.fold_in(_rk, 7), (4,), 0, max(1, 256 // 4) + 1, jnp.int32)
        _lenS2 = 256 - jax.random.randint(jax.random.fold_in(_rk, 8), (4,), 0, max(1, 256 // 4) + 1, jnp.int32)
        _ctx_1024P = jax.random.normal(jax.random.fold_in(_rk, 11), (4, 16, 128), jnp.float32)
        _ctx_1024c = jax.random.dirichlet(jax.random.fold_in(_rk, 511), 0.3 * jnp.ones((16,), jnp.float32), (4, 256))
        _ctx_1024t = jnp.einsum('bsk,bkd->bsd', _ctx_1024c, _ctx_1024P)
        _ctx_1024t = _ctx_1024t * jax.lax.rsqrt(jnp.mean(jnp.square(_ctx_1024t)) + 1e-12) * 0.953939
        ctx_1024 = 2.81802e-05 + 1.00001 * (_ctx_1024t + 0.3 * jax.random.normal(jax.random.fold_in(_rk, 611), (4, 256, 128), jnp.float32))
        return (x, ctx_1024)
    x, ctx_1024 = _rec_inputs()

    def _L0_attn_setup():
        import jax, jax.numpy as jnp
        import numpy as np
        D_MODEL = 256
        N_HEADS = 16
        HEAD_DIM = 128
        WINDOW = 64
        ROPE_BASE = 10000.0
        B, N = (2, 256)
        INNER = N_HEADS * HEAD_DIM

        def _rotate_half(t):
            t1, t2 = jnp.split(t, 2, axis=-1)
            return jnp.concatenate([-t2, t1], axis=-1)

        def _rope(q, k, offset=0):
            D = q.shape[-1]
            inv_freq = 1.0 / ROPE_BASE ** (jnp.arange(0, D, 2, dtype=jnp.float32) / D)
            pos = jnp.arange(q.shape[2], dtype=jnp.float32) + offset
            ang = pos[:, None] * inv_freq[None, :]
            cos = jnp.concatenate([jnp.cos(ang), jnp.cos(ang)], axis=-1)
            sin = jnp.concatenate([jnp.sin(ang), jnp.sin(ang)], axis=-1)
            q_r = q * cos + _rotate_half(q) * sin
            k_r = k * cos + _rotate_half(k) * sin
            return (q_r, k_r)
        key = jax.random.key(seed)
        k1, k2, k3 = jax.random.split(key, 3)
        x = jax.random.normal(k1, (B, N, D_MODEL), dtype=jnp.float32)
        w_qkv = jax.random.normal(k2, (3 * INNER, D_MODEL), dtype=jnp.float32) / np.sqrt(D_MODEL)
        w_o = jax.random.normal(k3, (D_MODEL, INNER), dtype=jnp.float32) / np.sqrt(INNER)
        return {'x': x, 'w_qkv': w_qkv, 'w_o': w_o}
    _L0_attn_all = _L0_attn_setup()
    _L0_attn_in = {k: v for k, v in _L0_attn_all.items() if k in ('w_qkv', 'w_o')}
    del _L0_attn_all

    def _L0_xattn_setup():
        import jax, jax.numpy as jnp
        import numpy as np
        key = jax.random.key(seed)
        ks = jax.random.split(key, 6)
        B, L, N, C, D = (8, 64, 256, 128, 128)
        return {'teacher_logits': jax.random.normal(ks[0], (B, L, N), dtype=jnp.float32), 'teacher_features': jax.random.normal(ks[1], (B, N, C), dtype=jnp.float32), 'Wq': jax.random.normal(ks[2], (D, C), dtype=jnp.float32) * (1.0 / np.sqrt(C)), 'bq': jnp.zeros((D,), dtype=jnp.float32), 'Wk': jax.random.normal(ks[3], (D, C), dtype=jnp.float32) * (1.0 / np.sqrt(C)), 'bk': jnp.zeros((D,), dtype=jnp.float32)}
    _L0_xattn_all = _L0_xattn_setup()
    _L0_xattn_in = {k: v for k, v in _L0_xattn_all.items() if k in ('Wq', 'bq', 'Wk', 'bk')}
    del _L0_xattn_all

    def _L0_ffn_setup():
        import jax, jax.numpy as jnp
        import numpy as np
        LORA_ALPHA = 16.0
        TOP_K = 2
        key = jax.random.key(seed)
        k_x, k_w, k_g, k_a, k_b = jax.random.split(key, 5)
        B, S, H, O, E, R = (2, 256, 256, 256, 8, 16)
        x = jax.random.normal(k_x, (B, S, H), dtype=jnp.float32)
        weight = jax.random.normal(k_w, (O, H), dtype=jnp.float32)
        gate_w = jax.random.normal(k_g, (E, H), dtype=jnp.float32) * 0.02
        A_w = jax.random.normal(k_a, (E, R, H), dtype=jnp.float32) * (1.0 / np.sqrt(H))
        B_w = jax.random.normal(k_b, (E, O, R), dtype=jnp.float32) * 0.01
        return {'x': x, 'weight': weight, 'gate_w': gate_w, 'A_w': A_w, 'B_w': B_w}
    _L0_ffn_all = _L0_ffn_setup()
    _L0_ffn_in = {k: v for k, v in _L0_ffn_all.items() if k in ('weight', 'gate_w', 'A_w', 'B_w')}
    del _L0_ffn_all
    return {'x': x, 'ctx_1024': ctx_1024, 'L0_attn_w_qkv': _L0_attn_in['w_qkv'], 'L0_attn_w_o': _L0_attn_in['w_o'], 'L0_xattn_Wq': _L0_xattn_in['Wq'], 'L0_xattn_bq': _L0_xattn_in['bq'], 'L0_xattn_Wk': _L0_xattn_in['Wk'], 'L0_xattn_bk': _L0_xattn_in['bk'], 'L0_ffn_weight': _L0_ffn_in['weight'], 'L0_ffn_gate_w': _L0_ffn_in['gate_w'], 'L0_ffn_A_w': _L0_ffn_in['A_w'], 'L0_ffn_B_w': _L0_ffn_in['B_w']}

def reference(x, ctx_1024, L0_attn_w_qkv, L0_attn_w_o, L0_xattn_Wq, L0_xattn_bq, L0_xattn_Wk, L0_xattn_bk, L0_ffn_weight, L0_ffn_gate_w, L0_ffn_A_w, L0_ffn_B_w):
    import jax
    import jax.numpy as jnp

    def _L0_attn_ref(x, w_qkv, w_o):
        import jax, jax.numpy as jnp
        import numpy as np
        D_MODEL = 256
        N_HEADS = 16
        HEAD_DIM = 128
        WINDOW = 64
        ROPE_BASE = 10000.0
        B, N = (2, 256)
        INNER = N_HEADS * HEAD_DIM

        def _rotate_half(t):
            t1, t2 = jnp.split(t, 2, axis=-1)
            return jnp.concatenate([-t2, t1], axis=-1)

        def _rope(q, k, offset=0):
            D = q.shape[-1]
            inv_freq = 1.0 / ROPE_BASE ** (jnp.arange(0, D, 2, dtype=jnp.float32) / D)
            pos = jnp.arange(q.shape[2], dtype=jnp.float32) + offset
            ang = pos[:, None] * inv_freq[None, :]
            cos = jnp.concatenate([jnp.cos(ang), jnp.cos(ang)], axis=-1)
            sin = jnp.concatenate([jnp.sin(ang), jnp.sin(ang)], axis=-1)
            q_r = q * cos + _rotate_half(q) * sin
            k_r = k * cos + _rotate_half(k) * sin
            return (q_r, k_r)
        Bq, Nq, _ = x.shape
        qkv = jnp.einsum('bnd,ed->bne', x, w_qkv)
        q, k, v = jnp.split(qkv, 3, axis=-1)

        def to_heads(t):
            return t.reshape(Bq, Nq, N_HEADS, HEAD_DIM).transpose(0, 2, 1, 3)
        q, k, v = (to_heads(q), to_heads(k), to_heads(v))
        q, k = _rope(q, k, offset=0)
        i = jnp.arange(Nq)[:, None]
        j = jnp.arange(Nq)[None, :]
        valid = (j > i - WINDOW) & (j <= i)
        scale = 1.0 / np.sqrt(HEAD_DIM)
        scores = jnp.einsum('bhnd,bhkd->bhnk', q, k) * scale
        scores = jnp.where(valid[None, None], scores, -jnp.inf)
        att = jax.nn.softmax(scores, axis=-1)
        out = jnp.einsum('bhnk,bhkd->bhnd', att, v)
        out = out.transpose(0, 2, 1, 3).reshape(Bq, Nq, INNER)
        y = jnp.einsum('bni,di->bnd', out, w_o)
        return y

    def _L0_xattn_ref(teacher_logits, teacher_features, Wq, bq, Wk, bk):
        import jax, jax.numpy as jnp
        import numpy as np
        query = jnp.einsum('bnc,dc->bnd', teacher_features, Wq) + bq
        key = jnp.einsum('bnc,dc->bnd', teacher_features, Wk) + bk
        energy = jnp.einsum('bnd,bmd->bnm', query, key)
        attention = jax.nn.softmax(energy, axis=-1)
        x_m = jnp.einsum('bln,bmn->blm', teacher_logits, attention)
        return x_m

    def _L0_ffn_ref(x, weight, gate_w, A_w, B_w):
        import jax, jax.numpy as jnp
        import numpy as np
        LORA_ALPHA = 16.0
        TOP_K = 2
        E = gate_w.shape[0]
        out = jnp.einsum('bsh,oh->bso', x, weight)
        logits = jnp.einsum('bsh,eh->bse', x, gate_w)
        probs = jax.nn.softmax(logits, axis=-1)
        topk_w, topk_idx = jax.lax.top_k(probs, TOP_K)
        topk_w = topk_w / jnp.sum(topk_w, axis=-1, keepdims=True)
        onehot = jax.nn.one_hot(topk_idx, E, dtype=x.dtype)
        cw = jnp.einsum('bsk,bske->bse', topk_w, onehot)
        t = jnp.einsum('bsh,erh->bser', x, A_w)
        t = t * cw[..., None]
        lora = jnp.einsum('bser,eor->bso', t, B_w)
        return out + LORA_ALPHA * lora
    x = _layernorm(x + _L0_attn_ref(x, L0_attn_w_qkv, L0_attn_w_o), axis=-1)
    x = _layernorm(x + _L0_xattn_ref(x, ctx_1024, L0_xattn_Wq, L0_xattn_bq, L0_xattn_Wk, L0_xattn_bk), axis=-1)
    x = _layernorm(x + _L0_ffn_ref(x, L0_ffn_weight, L0_ffn_gate_w, L0_ffn_A_w, L0_ffn_B_w), axis=-1)
    return x

_drawn_inputs = setup_inputs


def setup_inputs(seed=0):
    import zlib

    import numpy as np

    out = dict(_drawn_inputs(seed))
    spreads = {'L0_xattn_bq': (0.0, 0.1), 'L0_xattn_bk': (0.0, 0.1)}
    factors = {}
    for name, (base, spread) in spreads.items():
        noise = np.random.default_rng([zlib.crc32(name.encode()), seed]).standard_normal(out[name].shape)
        drawn = base * np.exp(spread * noise) if base else spread * noise
        out[name] = jnp.asarray(drawn.astype(out[name].dtype))
    for name, factor in factors.items():
        out[name] = (out[name] * factor).astype(out[name].dtype)
    return out
```

```python
from contextlib import ExitStack

import concourse.bass as bass
from concourse import mybir

F32 = mybir.dt.float32
F32R = mybir.dt.float32r
ALU = mybir.AluOpType
ACT = mybir.ActivationFunctionType
AX = mybir.AxisListType

P = 128
BATCH, SEQ, DM = 4, 256, 256
HEADS, HD, WINDOW = 16, 128, 64
CTX = 128
EXPERTS, RANK = 8, 16
LORA_ALPHA = 16.0
EPS = 1e-5
SCALE = float(HD) ** -0.5

TOK = BATCH * SEQ
KT = DM // P
TILES = TOK // P
GROUPS = HEADS // 2
SLOTS = 4
UNITS = GROUPS * SLOTS
PAIR = 2 * SEQ
S0 = SEQ // 2
S1 = SEQ - WINDOW
SW = S0 + S1
FW = DM + EXPERTS + EXPERTS * RANK
PIECE = 512
QK_H0, QK_H1, WV, WO = range(4)
LOADED = 16


def build(nc, x_nat, x_T, ctx_T, w_qk, w_v, w_o, xq_T, xk_T, x_bias, ffn_T, lora_bT,
          rope_cos, rope_sin, score_mask, identity, below, out):
    ctx = ExitStack()
    with ctx:
        def sb(name, shape, dt=F32):
            return ctx.enter_context(nc.sbuf_tensor(name, shape, dt))

        def bank(name):
            return ctx.enter_context(nc.psum_tensor(name, [P, 512], F32))

        def sem(name):
            return ctx.enter_context(nc.semaphore(name))

        x_hi = sb("x_hi", [P, KT, TOK], F32R)
        x_lo = sb("x_lo", [P, KT, TOK], F32R)
        acc = sb("acc", [P, TILES, DM])
        stage = sb("stage", [P, 4, PIECE])
        qk_hi = sb("qk_hi", [P, 2, 2, KT, HD], F32R)
        qk_lo = sb("qk_lo", [P, 2, 2, KT, HD], F32R)
        v_hi = sb("v_hi", [P, KT, HEADS * HD], F32R)
        v_lo = sb("v_lo", [P, KT, HEADS * HD], F32R)
        o_hi = sb("o_hi", [P, HEADS * DM], F32R)
        o_lo = sb("o_lo", [P, HEADS * DM], F32R)
        rope = sb("rope", [P, 4, PAIR])
        qr = sb("qr", [P, 2, PAIR])
        kr = sb("kr", [P, 2, PAIR])
        masked = sb("masked", [P, 2, SW])
        probs = sb("probs", [P, 2, S0 + SEQ])
        probs_T = sb("probs_T", [P, 2, SW])
        vals = sb("vals", [P, 2, 2, 2, 2 * HD])
        head_hi = sb("head_hi", [P, SLOTS, PAIR], F32R)
        head_lo = sb("head_lo", [P, SLOTS, PAIR], F32R)
        energy = sb("energy", [P, BATCH, 2, SEQ])
        mix_T = sb("mix_T", [P, BATCH, 2, SEQ])
        cosT = sb("cosT", [P, PAIR])
        sinT = sb("sinT", [P, PAIR])
        mask = sb("mask", [P, SW])
        ident = sb("ident", [P, P])
        xq_w = sb("xq_w", [P, CTX])
        xk_w = sb("xk_w", [P, CTX])
        xbias = sb("xbias", [P, 2])
        ffn_w = sb("ffn_w", [P, KT, FW])
        lora_b = sb("lora_b", [P, DM])
        tri = sb("tri", [P, EXPERTS * EXPERTS])
        nmin = sb("nmin", [P, 2, 2])
        carrier = sb("carrier", [1, 2 * SLOTS])
        rsum = sb("rsum", [P, 2, 2])
        rinv = sb("rinv", [P, 2, 2])
        xmax = sb("xmax", [P, BATCH, 2])
        xsum = sb("xsum", [P, BATCH, 2])
        xinv = sb("xinv", [P, BATCH, 2])
        stats = sb("stats", [P, BATCH, 2, 6])
        moments = sb("moments", [P, 3, BATCH, 2, 2])
        veps = sb("veps", [P, 3, BATCH, 2])
        rstd = sb("rstd", [P, 3, BATCH, 2])
        power = sb("power", [P, 2])
        logit = sb("logit", [P, BATCH, 2, EXPERTS])
        nlmax = sb("nlmax", [P, BATCH, 2])
        lexp = sb("lexp", [P, BATCH, 2, EXPERTS])
        above = sb("above", [P, BATCH, 2, EXPERTS * EXPERTS])
        equal = sb("equal", [P, BATCH, 2, EXPERTS * EXPERTS])
        rank = sb("rank", [P, BATCH, 2 * EXPERTS])
        chosen = sb("chosen", [P, BATCH, 2 * EXPERTS])
        gsum = sb("gsum", [P, BATCH, 2])
        ginv = sb("ginv", [P, BATCH, 2])
        gate = sb("gate", [P, BATCH, 2, EXPERTS])

        x_stage = rope[:, :, :].rearrange("p a n -> p (a n)").rearrange("p (k n) -> p k n", k=KT)
        ctx_sb = kr[:, :, :].rearrange("p a n -> p (a n)")
        flat_vals = vals[:, :, :, :, :].rearrange("p a b c n -> p (a b c n)")
        xq_sb, xk_sb = flat_vals[:, 0:TOK], flat_vals[:, TOK:2 * TOK]
        x1_T = energy
        x2 = rope[:, :, :].rearrange("p b (m n) -> p b m n", m=2)
        x2_T = stage[:, :, :].rearrange("p b (k n) -> p b k n", k=KT)
        lora_t = flat_vals[:, 0:TOK].rearrange("p (b m n) -> p b m n", b=BATCH, m=2)
        lora_tT = flat_vals[:, TOK:2 * TOK].rearrange("p (b n) -> p b n", b=BATCH)

        def final(b):
            return (qr if b < 2 else kr)[:, b % 2, :].rearrange("p (m n) -> p m n", m=2)

        bank_q, bank_k, bank_vy, bank_o = bank("bank_q"), bank("bank_k"), bank("bank_vy"), bank("bank_o")
        bank_s = [bank("bank_s0"), bank("bank_s1")]
        bank_t = [bank("bank_t0"), bank("bank_t1")]
        proj_bank = bank_s + bank_t
        bank_f = [[bank_s[0], bank_s[1]], [bank_o, bank_vy]]

        ctx_in, xT_in, tab_in, ffn_in = (sem(n) for n in ("ctx_in", "xT_in", "tab_in", "ffn_in"))
        piece_in = [sem(f"piece_in{i}") for i in range(4)]
        hi_done = [sem(f"hi_done{i}") for i in range(4)]
        lo_done = [sem(f"lo_done{i}") for i in range(4)]
        xhi_done, x_split = sem("xhi_done"), sem("x_split")
        zeroed = sem("zeroed")
        xproj_ready, xproj_copied = sem("xproj_ready"), sem("xproj_copied")
        energy_ready, xmax_done, xexp_done, xinv_done, energy_done = (
            sem(n) for n in ("energy_ready", "xmax_done", "xexp_done", "xinv_done", "energy_done"))
        mix_ready, mix_copied = sem("mix_ready"), sem("mix_copied")
        q_ready, k_ready, v_ready, v_copied = (sem(n) for n in ("q_ready", "k_ready", "v_ready", "v_copied"))
        q_scaled, k_scaled, q_rotated, k_rotated = (
            sem(n) for n in ("q_scaled", "k_scaled", "q_rotated", "k_rotated"))
        scores_ready, masked_done, exp_done, rinv_done, probs_done = (
            sem(n) for n in ("scores_ready", "masked_done", "exp_done", "rinv_done", "probs_done"))
        t_ready, t_copied, o_ready = sem("t_ready"), sem("t_copied"), sem("o_ready")
        head_hi_done, head_done = sem("head_hi_done"), sem("head_done")
        y_ready, y_added = sem("y_ready"), sem("y_added")
        ln_moments = [sem(f"ln_moments{i}") for i in range(3)]
        ln_stats, ln_veps = sem("ln_stats"), sem("ln_veps")
        ln_rstd = [sem(f"ln_rstd{i}") for i in range(3)]
        x1_done, x1T_ready, x1T_copied = sem("x1_done"), sem("x1T_ready"), sem("x1T_copied")
        xm_ready, x2_summed, x2_done, x2T_ready, x2T_copied = (
            sem(n) for n in ("xm_ready", "x2_summed", "x2_done", "x2T_ready", "x2T_copied"))
        ff_ready, logit_done, lexp_done, gate_step, lora_done = (
            sem(n) for n in ("ff_ready", "logit_done", "lexp_done", "gate_step", "lora_done"))
        lT_ready, lT_copied, f_ready, x3_summed, x3_done = (
            sem(n) for n in ("lT_ready", "lT_copied", "f_ready", "x3_summed", "x3_done"))
        out_done = sem("out_done")

        def back(it, slot, n):
            turns, slot = divmod(slot - n, SLOTS)
            return (it + turns if turns else it), slot

        def present(it, slot, n):
            return not isinstance(it, int) or 0 <= SLOTS * it + slot - n < UNITS

        def first(it):
            return isinstance(it, int) and it == 0

        def wait(eng, semaphore, it, slot, each, plus):
            value = it * (each * SLOTS) + (each * slot + plus)
            if not isinstance(value, int) or value > 0:
                eng.wait_ge(semaphore, value)

        def wait_group(eng, semaphore, it, plus, each=1):
            value = it * each + plus
            if not isinstance(value, int) or value > 0:
                eng.wait_ge(semaphore, value)

        def all_steps(eng, step):
            for slot in range(SLOTS):
                step(0, slot)
            with nc.allow_low_precision("float32r parts are exact"):
                with eng.Fori(1, GROUPS - 1) as it:
                    for slot in range(SLOTS):
                        step(it, slot)
            for slot in range(SLOTS + 4):
                step(GROUPS - 1, slot)

        def staged(piece):
            if piece == WV:
                return stage[:, piece, :].rearrange("p (k n) -> p k n", k=KT)
            return stage[:, piece, :]

        def weight_part(piece, g, part):
            if piece == WV:
                return (v_hi, v_lo)[part][:, :, bass.ds(g * (2 * HD), 2 * HD)]
            if piece == WO:
                return (o_hi, o_lo)[part][:, bass.ds(g * (2 * DM), 2 * DM)]
            return (qk_hi, qk_lo)[part][:, piece, :, :, :].rearrange("p a k n -> p (a k n)")

        block = ctx.enter_context(nc.Block())

        @block.sync
        def _(sp):
            sp.dma_start(ctx_sb, ctx_T).then_inc(ctx_in, 16)
            sp.dma_start(xq_w[:, :], xq_T).then_inc(ctx_in, 16)
            sp.dma_start(xk_w[:, :], xk_T).then_inc(ctx_in, 16)
            sp.dma_start(xbias[:, :], x_bias).then_inc(ctx_in, 16)
            sp.dma_start(x_stage, x_T).then_inc(xT_in, 16)

            def load(piece, g):
                src = (w_qk[g, :, 0:PIECE], w_qk[g, :, PIECE:2 * PIECE], w_v[g, :, :], w_o[g, :, :])[piece]
                sp.dma_start(stage[:, piece, :], src).then_inc(piece_in[piece], 16)

            def reload(piece, g, plus):
                wait_group(sp, lo_done[piece], g, plus)
                load(piece, g + plus)

            load(QK_H0, 0)
            sp.dma_start(cosT[:, :], rope_cos).then_inc(tab_in, 16)
            sp.dma_start(sinT[:, :], rope_sin).then_inc(tab_in, 16)
            load(WV, 0)
            load(QK_H1, 0)
            sp.dma_start(mask[:, :], score_mask).then_inc(tab_in, 16)
            sp.dma_start(ident[:, :], identity).then_inc(tab_in, 16)
            load(WO, 0)
            sp.dma_start(acc[:, :, :], x_nat).then_inc(y_added, LOADED)
            sp.dma_start(ffn_w[:, :, :], ffn_T).then_inc(ffn_in, 16)
            sp.dma_start(lora_b[:, :], lora_bT).then_inc(ffn_in, 16)
            sp.dma_start(tri[:, :], below).then_inc(ffn_in, 16)
            reload(QK_H0, 0, 1)
            reload(WV, 0, 1)
            with sp.Fori(0, GROUPS - 2) as g:
                for piece, plus in ((QK_H1, 1), (WO, 1), (WV, 2), (QK_H0, 2)):
                    reload(piece, g, plus)
            for piece in (QK_H1, WO):
                reload(piece, GROUPS - 2, 1)
            for b in range(BATCH):
                sp.wait_ge(x3_done, 2 * (b + 1))
                sp.dma_start(out[:, 2 * b:2 * b + 2, :], final(b)).then_inc(out_done, 16)
            sp.wait_ge(out_done, 16 * BATCH)

        @block.tensor
        def _(pe):
            def three_passes(dst, w, x, first, last):
                for n, (a, b) in enumerate(((0, 0), (0, 1), (1, 0))):
                    mm = pe.matmul(dst, w[a], x[b], start=first and n == 0, stop=last and n == 2)
                return mm

            def project(dst, what, slot):
                pair, j = divmod(slot, 2)
                for k in range(KT):
                    mm = three_passes(dst[:, :], (qk_hi[:, j, what, k, :], qk_lo[:, j, what, k, :]),
                                      (x_hi[:, k, pair * PAIR:(pair + 1) * PAIR],
                                       x_lo[:, k, pair * PAIR:(pair + 1) * PAIR]), k == 0, k == KT - 1)
                return mm

            def q_project(it, slot):
                wait_group(pe, lo_done[slot % 2], it, 1)
                wait(pe, q_scaled, it, slot, 1, 0)
                project(bank_q, 0, slot).then_inc(q_ready, 1)

            def k_project(it, slot):
                wait(pe, k_scaled, it, slot, 1, 0)
                project(bank_k, 1, slot).then_inc(k_ready, 1)

            def v_project(it, slot):
                wait_group(pe, lo_done[WV], it, 1)
                if not first(it):
                    wait(pe, y_added, it, slot, 1, LOADED - 4)
                for m in range(2):
                    tok = slot * SEQ + m * P
                    for k in range(KT):
                        rhs = [v[:, k, bass.ds(it * (2 * HD), 2 * HD)] for v in (v_hi, v_lo)]
                        mm = three_passes(bank_vy[:, m * 2 * HD:(m + 1) * 2 * HD],
                                          (x_hi[:, k, tok:tok + P], x_lo[:, k, tok:tok + P]),
                                          rhs, k == 0, k == KT - 1)
                mm.then_inc(v_ready, 1)

            def scores(it, slot):
                wait(pe, q_rotated, it, slot, 1, 1)
                wait(pe, k_rotated, it, slot, 1, 1)
                q, k = qr[:, slot % 2, :], kr[:, slot % 2, :]
                for b in range(2):
                    wait(pe, masked_done, it, slot, 2, b - 1)
                    o = b * SEQ
                    pe.matmul(bank_s[b][:, 0:S0], q[:, o:o + P], k[:, o:o + P], start=True, stop=True)
                    pe.matmul(bank_s[b][:, S0:SW], q[:, o + P:o + SEQ], k[:, o + WINDOW:o + SEQ],
                              start=True, stop=True).then_inc(scores_ready, 1)

            def transposes(it, slot):
                for b in range(2):
                    wait(pe, probs_done, it, slot, 2, b + 1)
                    wait(pe, t_copied, it, slot, 2, b - 1)
                    t, p = bank_t[b], probs[:, b, :]
                    pe.transpose(t[:, 0:P], p[:, 0:P], ident[:, :])
                    pe.transpose(t[:, P:P + WINDOW], p[0:WINDOW, P:2 * P], ident[0:WINDOW, 0:WINDOW])
                    pe.transpose(t[:, P + WINDOW:SW], p[:, 2 * P:3 * P], ident[:, :]).then_inc(t_ready, 1)

            def attend(it, slot):
                pair, j = divmod(slot, 2)
                wait(pe, head_done, it, slot, 1, 0)
                for b in range(2):
                    wait(pe, v_copied, it, 2 * pair, 1, b + 1)
                    wait(pe, t_copied, it, slot, 2, b + 1)
                    o = b * SEQ
                    v = vals[:, pair, b, :, j * HD:(j + 1) * HD]
                    pe.matmul(bank_o[:, o:o + P + WINDOW], v[:, 0, :], probs_T[:, b, 0:P + WINDOW],
                              start=True, stop=False, skip_group_check=True)
                    pe.matmul(bank_o[:, o + P:o + SEQ], v[:, 1, :], probs_T[:, b, P + WINDOW:SW],
                              start=False, stop=True, skip_group_check=True).then_inc(o_ready, 1)

            def out_project(it, slot):
                pair, b = divmod(slot, 2)
                wait_group(pe, lo_done[WO], it, 1)
                wait(pe, head_done, it, 2 * pair, 1, 2)
                if present(it, slot, -4):
                    wait(pe, v_copied, *back(it, slot, -4), 1, 1)
                else:
                    wait(pe, y_added, it, slot, 1, LOADED)
                for m in range(2):
                    c = b * SEQ + m * P
                    for j in range(2):
                        rhs = [w[:, bass.ds(it * (2 * DM) + j * DM, DM)] for w in (o_hi, o_lo)]
                        mm = three_passes(bank_vy[:, m * DM:(m + 1) * DM],
                                          (head_hi[:, 2 * pair + j, c:c + P], head_lo[:, 2 * pair + j, c:c + P]),
                                          rhs, j == 0, j == 1)
                mm.then_inc(y_ready, 1)

            def step(it, slot):
                if present(it, slot, 0):
                    q_project(it, slot)
                    k_project(it, slot)
                if present(it, slot, 2):
                    transposes(*back(it, slot, 2))
                if first(it) and slot == 0:
                    cross_energy()
                if present(it, slot, 0):
                    v_project(it, slot)
                if present(it, slot, 2):
                    attend(*back(it, slot, 2))
                if first(it) and slot == 1:
                    cross_transposes()
                    pe.wait_ge(mix_copied, BATCH)
                if present(it, slot, 1):
                    scores(*back(it, slot, 1))
                if present(it, slot, 4):
                    out_project(*back(it, slot, 4))

            def cross_project():
                pe.wait_ge(ctx_in, 64)
                for n in range(4):
                    w, o = (xq_w, xk_w)[n // 2], (n % 2) * PAIR
                    pe.matmul(proj_bank[n][:, :], w[:, :], ctx_sb[:, o:o + PAIR],
                              start=True, stop=True).then_inc(xproj_ready, 1)

            def cross_energy():
                pe.wait_ge(xproj_copied, 4)
                for b in range(BATCH):
                    for m in range(2):
                        o = b * SEQ
                        mm = pe.matmul(proj_bank[b][:, m * SEQ:(m + 1) * SEQ],
                                       xq_sb[:, o + m * P:o + (m + 1) * P], xk_sb[:, o:o + SEQ],
                                       start=True, stop=True)
                    mm.then_inc(energy_ready, 1)

            def cross_transposes():
                for b in range(BATCH):
                    pe.wait_ge(energy_done, b + 1)
                    for k in range(2):
                        for m in range(2):
                            c = k * SEQ + m * P
                            mm = pe.transpose(proj_bank[b][:, c:c + P], energy[:, b, m, k * P:(k + 1) * P],
                                              ident[:, :])
                    mm.then_inc(mix_ready, 1)

            cross_project()
            pe.wait_ge(x_split, 2)
            pe.wait_ge(tab_in, 64)
            all_steps(pe, step)

            def x1_transposes(b):
                pe.wait_ge(x1_done, 2 * (b + 1))
                if b:
                    pe.wait_ge(x1T_copied, b)
                for k in range(KT):
                    for m in range(2):
                        mm = pe.transpose(bank_q[:, k * SEQ + m * P:k * SEQ + (m + 1) * P],
                                          acc[:, 2 * b + m, k * P:(k + 1) * P], ident[:, :])
                mm.then_inc(x1T_ready, 1)

            def cross_mix(b):
                pe.wait_ge(x1T_copied, b + 1)
                if b:
                    pe.wait_ge(x2_summed, b)
                for m in range(2):
                    for k in range(KT):
                        mm = pe.matmul(bank_k[:, m * SEQ:(m + 1) * SEQ], x1_T[:, b, k, m * P:(m + 1) * P],
                                       mix_T[:, b, k, :], start=(k == 0), stop=(k == KT - 1))
                mm.then_inc(xm_ready, 1)

            def x2_transposes(b):
                pe.wait_ge(x2_done, 2 * (b + 1))
                if b:
                    pe.wait_ge(x2T_copied, b)
                for k in range(KT):
                    for m in range(2):
                        mm = pe.transpose(bank_t[0][:, k * SEQ + m * P:k * SEQ + (m + 1) * P],
                                          x2[:, b, m, k * P:(k + 1) * P], ident[:, :])
                mm.then_inc(x2T_ready, 1)

            def feed_forward(b):
                pe.wait_ge(x2T_copied, b + 1)
                if b == 0:
                    pe.wait_ge(ffn_in, 48)
                if b == 1:
                    pe.wait_ge(y_added, LOADED + UNITS)
                if b >= 2:
                    pe.wait_ge(x3_summed, 2 * (b - 1))
                for m in range(2):
                    for k in range(KT):
                        mm = pe.matmul(bank_f[b % 2][m][:, 0:FW], x2_T[:, b, k, m * P:(m + 1) * P],
                                       ffn_w[:, k, :], start=(k == 0), stop=(k == KT - 1),
                                       skip_group_check=True)
                mm.then_inc(ff_ready, 1)

            def lora_transposes(b):
                pe.wait_ge(lora_done, 2 * (b + 1))
                if b:
                    pe.wait_ge(lT_copied, b)
                for m in range(2):
                    mm = pe.transpose(bank_t[1][:, m * P:(m + 1) * P], lora_t[:, b, m, :], ident[:, :])
                mm.then_inc(lT_ready, 1)

            def lora_add(b):
                pe.wait_ge(lT_copied, b + 1)
                for m in range(2):
                    mm = pe.matmul(bank_f[b % 2][m][:, 0:DM], lora_tT[:, b, m * P:(m + 1) * P],
                                   lora_b[:, :], start=False, stop=True, skip_group_check=True)
                mm.then_inc(f_ready, 1)

            stages = (x1_transposes, cross_mix, x2_transposes, feed_forward, lora_transposes, lora_add)
            for t in range(BATCH + len(stages) - 1):
                for n in reversed(range(len(stages))):
                    if 0 <= t - n < BATCH:
                        stages[n](t - n)

        @block.vector
        def _(dve):
            def q_scale(it, slot):
                rotate(it, slot, q_ready, q_rotated, bank_q, 0).then_inc(q_scaled, 1)

            def k_scale(it, slot):
                rotate(it, slot, k_ready, k_rotated, bank_k, 2).then_inc(k_scaled, 1)

            def rotate(it, slot, ready, rotated, src, n):
                wait(dve, ready, it, slot, 1, 1)
                wait(dve, rotated, it, slot, 1, 0)
                h = HD // 2
                dve.tensor_tensor(rope[:, n, :], src[:, :], cosT[:, :], ALU.mult)
                dve.tensor_tensor(rope[0:h, n + 1, :], src[h:HD, :], sinT[h:HD, :], ALU.mult)
                return dve.tensor_tensor(rope[h:HD, n + 1, :], src[0:h, :], sinT[0:h, :], ALU.mult)

            def mask_and_max(it, slot):
                for b in range(2):
                    wait(dve, scores_ready, it, slot, 2, b + 1)
                    wait(dve, exp_done, it, slot, 2, b - 1)
                    dve.memset(carrier[0:1, 2 * slot + b:2 * slot + b + 1], 0.0)
                    for t, (a, z) in enumerate(((0, S0), (S0, SW))):
                        last = dve.tensor_tensor_reduce(masked[:, b, a:z], bank_s[b][:, a:z], mask[:, a:z],
                                                        -SCALE, 3e38, ALU.add, ALU.min, nmin[:, b, t:t + 1])
                    last.then_inc(masked_done, 1)

            def normalise(it, slot):
                for b in range(2):
                    wait(dve, exp_done, it, slot, 2, b + 1)
                    dve.reciprocal(rinv[:, b, :], rsum[:, b, :]).then_inc(rinv_done, 1)
                    wait(dve, rinv_done, it, slot, 2, b + 1)
                    dve.tensor_scalar(probs[:, b, 0:S0], probs[:, b, 0:S0], rinv[:, b, 0:1], None, ALU.mult)
                    dve.tensor_scalar(probs[:, b, P + WINDOW:], probs[:, b, P + WINDOW:], rinv[:, b, 1:2],
                                      None, ALU.mult).then_inc(probs_done, 1)

            def head_low(it, slot):
                wait(dve, head_hi_done, it, slot, 1, 1)
                dve.tensor_tensor(head_lo[:, slot, :], bank_o[:, :], head_hi[:, slot, :].bitcast(F32),
                                  ALU.subtract).then_inc(head_done, 1)

            def add_output(it, slot):
                wait(dve, y_ready, it, slot, 1, 1)
                wait(dve, y_added, it, slot, 1, LOADED)
                rows = acc[:, 2 * slot:2 * slot + 2, :].rearrange("p m n -> p (m n)")
                dve.tensor_tensor(rows, bank_vy[:, :], rows, ALU.add).then_inc(y_added, 1)

            def cross_max(b):
                dve.wait_ge(energy_ready, b + 1)
                dve.tensor_reduce(xmax[:, b, :], proj_bank[b][:, :].rearrange("p (m n) -> p m n", m=2),
                                  AX.X, ALU.max, negate=True).then_inc(xmax_done, 1)

            def cross_normalise(b):
                dve.wait_ge(xexp_done, b + 1)
                dve.reciprocal(xinv[:, b, :], xsum[:, b, :]).then_inc(xinv_done, 1)
                dve.wait_ge(xinv_done, b + 1)
                for m in range(2):
                    last = dve.tensor_scalar(energy[:, b, m, :], energy[:, b, m, :], xinv[:, b, m:m + 1],
                                             None, ALU.mult)
                last.then_inc(energy_done, 1)

            def step(it, slot):
                if present(it, slot, 0):
                    q_scale(it, slot)
                    k_scale(it, slot)
                if first(it) and slot == 0:
                    for b in range(BATCH):
                        cross_max(b)
                    for b in range(BATCH):
                        cross_normalise(b)
                if present(it, slot, 2):
                    head_low(*back(it, slot, 2))
                if present(it, slot, 1):
                    mask_and_max(*back(it, slot, 1))
                if present(it, slot, 4):
                    add_output(*back(it, slot, 4))
                if present(it, slot, 1):
                    normalise(*back(it, slot, 1))

            for b in range(2):
                dve.memset(probs[:, b, P:P + WINDOW], 0.0).then_inc(zeroed, 1)
            dve.memset(power[:, :], -0.5).then_inc(zeroed, 1)
            dve.wait_ge(xT_in, 16)
            for c in range(2):
                part = slice(c * PAIR, (c + 1) * PAIR)
                dve.tensor_copy(x_hi[:, :, part], x_stage[:, :, part]).then_inc(xhi_done, 1)
            for c in range(2):
                part = slice(c * PAIR, (c + 1) * PAIR)
                dve.wait_ge(xhi_done, c + 1)
                dve.tensor_tensor(x_lo[:, :, part], x_stage[:, :, part], x_hi[:, :, part].bitcast(F32),
                                  ALU.subtract).then_inc(x_split, 1)
            dve.wait_ge(x_split, 2)
            dve.wait_ge(tab_in, 64)
            all_steps(dve, step)

            self_count = [0]

            def norm_stats(n, b, tiles):
                for m in range(2):
                    dve.bn_stats(stats[:, b, m, :], tiles[:, m, :]).then_inc(ln_stats, 1)
                    self_count[0] += 1
                dve.wait_ge(ln_stats, self_count[0])
                for m in range(2):
                    last = dve.bn_aggr(moments[:, n, b, m, :], stats[:, b, m, :])
                last.then_inc(ln_moments[n], 1)

            def norm_apply(n, b, tiles, done):
                dve.wait_ge(ln_rstd[n], b + 1)
                for m in range(2):
                    dve.tensor_scalar(tiles[:, m, :], tiles[:, m, :], moments[:, n, b, m, 0:1],
                                      rstd[:, n, b, m:m + 1], ALU.subtract, ALU.mult).then_inc(done, 1)

            def ln1(b):
                tiles = acc[:, 2 * b:2 * b + 2, :]
                dve.wait_ge(y_added, LOADED + UNITS - BATCH + b + 1)
                norm_stats(0, b, tiles)
                norm_apply(0, b, tiles, x1_done)

            def ln2(b):
                dve.wait_ge(xm_ready, b + 1)
                dve.wait_ge(x1_done, 2 * (b + 1))
                dve.tensor_tensor(x2[:, b, :, :], bank_k[:, :].rearrange("p (m n) -> p m n", m=2),
                                  acc[:, 2 * b:2 * b + 2, :], ALU.add).then_inc(x2_summed, 1)
                dve.wait_ge(x2_summed, b + 1)
                norm_stats(1, b, x2[:, b, :, :])
                norm_apply(1, b, x2[:, b, :, :], x2_done)

            gates = [0]

            def own(instruction):
                gates[0] += 1
                instruction.then_inc(gate_step, 1)
                dve.wait_ge(gate_step, gates[0])

            def gating(b):
                f, e8 = bank_f[b % 2], EXPERTS
                dve.wait_ge(ff_ready, b + 1)
                for m in range(2):
                    dve.tensor_copy(logit[:, b, m, :], f[m][:, DM:DM + e8]).then_inc(logit_done, 1)
                dve.wait_ge(logit_done, 4 * b + 2)
                dve.tensor_reduce(nlmax[:, b, :], logit[:, b, :, :], AX.X, ALU.max,
                                  negate=True).then_inc(logit_done, 2)
                other = logit[:, b, :, :].unsqueeze(2).to_broadcast([P, 2, e8, e8])
                mine = logit[:, b, :, :].unsqueeze(3).to_broadcast([P, 2, e8, e8])
                gt = above[:, b, :, :].rearrange("p m (e f) -> p m e f", f=e8)
                eq = equal[:, b, :, :].rearrange("p m (e f) -> p m e f", f=e8)
                dve.tensor_tensor(eq, other, mine, ALU.is_equal)
                own(dve.tensor_tensor(gt, other, mine, ALU.is_gt))
                own(dve.tensor_tensor(equal[:, b, :, :], equal[:, b, :, :],
                                      tri[:, :].unsqueeze(1).to_broadcast([P, 2, e8 * e8]), ALU.mult))
                own(dve.tensor_tensor(above[:, b, :, :], above[:, b, :, :], equal[:, b, :, :], ALU.add))
                own(dve.tensor_reduce(rank[:, b, :], above[:, b, :, :].rearrange("p m (e f) -> p (m e) f", f=e8),
                                      AX.X, ALU.add))
                dve.wait_ge(lexp_done, b + 1)
                own(dve.scalar_tensor_tensor(chosen[:, b, :], rank[:, b, :], 1.5,
                                             lexp[:, b, :, :].rearrange("p m e -> p (m e)"), ALU.is_lt, ALU.mult))
                picked = chosen[:, b, :].rearrange("p (m e) -> p m e", m=2)
                own(dve.tensor_reduce(gsum[:, b, :], picked, AX.X, ALU.add))
                own(dve.reciprocal(ginv[:, b, :], gsum[:, b, :]))
                own(dve.scalar_tensor_tensor(gate[:, b, :, :], picked, LORA_ALPHA,
                                             ginv[:, b, :].unsqueeze(2).to_broadcast([P, 2, e8]),
                                             ALU.mult, ALU.mult))
                for m in range(2):
                    dve.tensor_tensor(lora_t[:, b, m, :].rearrange("p (e r) -> p e r", e=e8),
                                      f[m][:, DM + e8:FW].rearrange("p (e r) -> p e r", e=e8),
                                      gate[:, b, m, :].unsqueeze(2).to_broadcast([P, e8, RANK]),
                                      ALU.mult).then_inc(lora_done, 1)

            def ln3(b):
                dve.wait_ge(f_ready, b + 1)
                dve.wait_ge(x2_done, 2 * (b + 1))
                for m in range(2):
                    dve.tensor_tensor(final(b)[:, m, :], bank_f[b % 2][m][:, 0:DM], x2[:, b, m, :],
                                      ALU.add).then_inc(x3_summed, 1)
                dve.wait_ge(x3_summed, 2 * (b + 1))
                norm_stats(2, b, final(b))
                norm_apply(2, b, final(b), x3_done)

            for t in range(BATCH + 5):
                for stage_of, behind in ((ln1, 0), (ln3, 5), (gating, 3), (ln2, 1)):
                    if 0 <= t - behind < BATCH:
                        stage_of(t - behind)

        @block.scalar
        def _(act):
            def weight_high(piece, g, reuse=None):
                wait_group(act, piece_in[piece], g, 16, 16)
                if reuse is not None:
                    wait_group(act, k_ready, g, reuse, SLOTS)
                act.activation(weight_part(piece, g, 0), staged(piece), ACT.Copy).then_inc(hi_done[piece], 1)

            def copy_probs(it, slot):
                for b in range(2):
                    wait(act, t_ready, it, slot, 2, b + 1)
                    wait(act, o_ready, it, slot, 2, b - 1)
                    act.activation(probs_T[:, b, :], bank_t[b][:, 0:SW], ACT.Copy).then_inc(t_copied, 1)

            def head_high(it, slot):
                wait(act, o_ready, it, slot, 2, 2)
                if not first(it):
                    wait(act, y_added, it, 2 * (slot // 2), 1, LOADED - 2)
                act.activation(head_hi[:, slot, :], bank_o[:, :], ACT.Copy).then_inc(head_hi_done, 1)

            def exps(it, slot):
                for b in range(2):
                    wait(act, masked_done, it, slot, 2, b + 1)
                    wait(act, t_ready, it, slot, 2, b - 1)
                    act.activation(probs[:, b, 0:S0], masked[:, b, 0:S0], ACT.Exp, bias=nmin[:, b, 0:1],
                                   scale=-1.0, accum_out=rsum[:, b, 0:1])
                    act.activation(probs[:, b, P + WINDOW:], masked[:, b, S0:SW], ACT.Exp, bias=nmin[:, b, 1:2],
                                   scale=-1.0, accum_out=rsum[:, b, 1:2]).then_inc(exp_done, 1)

            def copy_values(it, slot):
                pair, b = divmod(slot, 2)
                wait(act, v_ready, it, slot, 1, 1)
                wait(act, o_ready, it, 2 * pair, 2, -4)
                act.activation(vals[:, pair, b, :, :].rearrange("p m n -> p (m n)"), bank_vy[:, :],
                               ACT.Copy).then_inc(v_copied, 1)

            def step(it, slot):
                if present(it, slot, 2):
                    copy_probs(*back(it, slot, 2))
                if present(it, slot, 0):
                    copy_values(it, slot)
                if slot < SLOTS:
                    if slot == 0:
                        weight_high(QK_H1, it, 0)
                    if slot == 1:
                        weight_high(WO, it)
                    if slot == 2 and present(it, slot, -4):
                        weight_high(WV, it + 1)
                    if slot == 3 and present(it, slot, -4):
                        weight_high(QK_H0, it + 1, -1)
                if present(it, slot, 2):
                    head_high(*back(it, slot, 2))
                if first(it) and slot == 0:
                    cross_exps()
                if first(it) and slot == 1:
                    copy_mix()
                if present(it, slot, 1):
                    exps(*back(it, slot, 1))

            def cross_exps():
                for b in range(BATCH):
                    act.wait_ge(xmax_done, b + 1)
                    for m in range(2):
                        last = act.activation(energy[:, b, m, :], proj_bank[b][:, m * SEQ:(m + 1) * SEQ], ACT.Exp,
                                              bias=xmax[:, b, m:m + 1], accum_out=xsum[:, b, m:m + 1])
                    last.then_inc(xexp_done, 1)

            def copy_mix():
                for b in range(BATCH):
                    act.wait_ge(mix_ready, b + 1)
                    act.activation(mix_T[:, b, :, :].rearrange("p k n -> p (k n)"), proj_bank[b][:, :],
                                   ACT.Copy).then_inc(mix_copied, 1)

            for n in range(4):
                act.wait_ge(xproj_ready, n + 1)
                dst, o = (xq_sb, xk_sb)[n // 2], (n % 2) * PAIR
                act.activation(dst[:, o:o + PAIR], proj_bank[n][:, :], ACT.Identity,
                               bias=xbias[:, n // 2:n // 2 + 1]).then_inc(xproj_copied, 1)
            weight_high(QK_H0, 0)
            weight_high(WV, 0)
            act.wait_ge(zeroed, 3)
            all_steps(act, step)

            def copy_x1T(b):
                act.wait_ge(x1T_ready, b + 1)
                act.activation(x1_T[:, b, :, :].rearrange("p k n -> p (k n)"), bank_q[:, :],
                               ACT.Copy).then_inc(x1T_copied, 1)

            def copy_x2T(b):
                act.wait_ge(x2T_ready, b + 1)
                act.activation(x2_T[:, b, :, :].rearrange("p k n -> p (k n)"), bank_t[0][:, :],
                               ACT.Copy).then_inc(x2T_copied, 1)

            def gate_exps(b):
                act.wait_ge(logit_done, 4 * b + 4)
                for m in range(2):
                    last = act.activation(lexp[:, b, m, :], logit[:, b, m, :], ACT.Exp, bias=nlmax[:, b, m:m + 1])
                last.then_inc(lexp_done, 1)

            def copy_loraT(b):
                act.wait_ge(lT_ready, b + 1)
                act.activation(lora_tT[:, b, :], bank_t[1][:, 0:SEQ], ACT.Copy).then_inc(lT_copied, 1)

            for t in range(BATCH + 4):
                for stage_of, behind in ((copy_loraT, 4), (gate_exps, 3), (copy_x2T, 2), (copy_x1T, 0)):
                    if 0 <= t - behind < BATCH:
                        stage_of(t - behind)

        @block.gpsimd
        def _(pool):
            def weight_low(piece, g):
                wait_group(pool, hi_done[piece], g, 1)
                pool.tensor_tensor(weight_part(piece, g, 1), staged(piece), weight_part(piece, g, 0).bitcast(F32),
                                   ALU.subtract).then_inc(lo_done[piece], 1)

            def rotate(it, slot, scaled, n, dst, rotated):
                wait(pool, scaled, it, slot, 1, 1)
                wait(pool, scores_ready, it, slot, 2, -2)
                pool.tensor_tensor(dst[:, slot % 2, :], rope[:, n, :], rope[:, n + 1, :],
                                   ALU.add).then_inc(rotated, 1)

            def step(it, slot):
                if present(it, slot, 0):
                    rotate(it, slot, q_scaled, 0, qr, q_rotated)
                    rotate(it, slot, k_scaled, 2, kr, k_rotated)
                if slot < SLOTS:
                    if slot == 0:
                        weight_low(QK_H1, it)
                    if slot == 1:
                        weight_low(WO, it)
                    if slot == 2 and present(it, slot, -4):
                        weight_low(WV, it + 1)
                    if slot == 3 and present(it, slot, -4):
                        weight_low(QK_H0, it + 1)

            weight_low(QK_H0, 0)
            weight_low(WV, 0)
            all_steps(pool, step)

            count = 0

            def inverse_std(n, b):
                nonlocal count
                pool.wait_ge(ln_moments[n], b + 1)
                pool.tensor_scalar(veps[:, n, b, :], moments[:, n, b, :, 1], EPS, None, ALU.add).then_inc(ln_veps, 1)
                count += 1
                pool.wait_ge(ln_veps, count)
                pool.tensor_tensor(rstd[:, n, b, :], veps[:, n, b, :], power[:, :], ALU.pow).then_inc(ln_rstd[n], 1)

            pool.wait_ge(zeroed, 3)
            for t in range(BATCH + 5):
                for n, behind in ((0, 0), (2, 5), (1, 1)):
                    if 0 <= t - behind < BATCH:
                        inverse_std(n, t - behind)


def kernel(**inputs):
    import numpy as np
    import concourse.bacc as bacc
    from concourse.bass_utils import run_bass_kernel_spmd

    f32 = np.float32
    a = {k: np.asarray(v) for k, v in inputs.items()}
    x = a["x"].reshape(TOK, DM)
    wqkv, inner = a["L0_attn_w_qkv"], HEADS * HD

    qk = wqkv[:2 * inner].reshape(2, GROUPS, 2, HD, KT, P)
    v = wqkv[2 * inner:].reshape(GROUPS, 2 * HD, KT, P)
    o = a["L0_attn_w_o"].reshape(DM, GROUPS, 2, HD)
    lay = {
        "x_nat": x.reshape(TILES, P, DM).transpose(1, 0, 2),
        "x_T": x.reshape(TOK, KT, P).transpose(2, 1, 0),
        "ctx_T": a["ctx_1024"].reshape(TOK, CTX).T,
        "w_qk": qk.transpose(1, 5, 2, 0, 4, 3).reshape(GROUPS, P, 2 * PIECE),
        "w_v": v.transpose(0, 3, 2, 1).reshape(GROUPS, P, PIECE),
        "w_o": o.transpose(1, 3, 2, 0).reshape(GROUPS, P, PIECE),
        "xq_T": a["L0_xattn_Wq"].T,
        "xk_T": a["L0_xattn_Wk"].T,
        "x_bias": np.stack([a["L0_xattn_bq"], a["L0_xattn_bk"]], axis=1),
        "ffn_T": np.concatenate([a["L0_ffn_weight"], a["L0_ffn_gate_w"],
                                 a["L0_ffn_A_w"].reshape(EXPERTS * RANK, DM)], axis=0)
                   .reshape(FW, KT, P).transpose(2, 1, 0),
        "lora_bT": a["L0_ffn_B_w"].transpose(0, 2, 1).reshape(EXPERTS * RANK, DM),
    }

    half = HD // 2
    inv_freq = (f32(1.0) / f32(10000.0) ** (np.arange(0, HD, 2, dtype=f32) / f32(HD))).astype(f32)
    angle = inv_freq[:, None] * np.arange(SEQ, dtype=f32)[None, :]
    cos, sin = np.cos(angle).astype(f32), np.sin(angle).astype(f32)
    query = np.arange(P)[:, None]
    key0, key1 = np.arange(S0)[None, :], np.arange(WINDOW, SEQ)[None, :]
    seen = np.concatenate([(key0 <= query) & (key0 > query - WINDOW),
                           (key1 <= query + P) & (key1 > query + P - WINDOW)], axis=1)
    expert = np.arange(EXPERTS)
    lay |= {
        "rope_cos": np.tile(np.concatenate([cos, cos]), (1, 2)),
        "rope_sin": np.tile(np.concatenate([sin, -sin]), (1, 2)),
        "score_mask": np.where(seen, f32(0), f32(-1e30)),
        "identity": np.eye(P, dtype=f32),
        "below": np.tile((expert[None, :] < expert[:, None]).astype(f32).reshape(1, -1), (P, 1)),
    }

    nc = bacc.Bacc("TRN2", target_bir_lowering=False, num_devices=1)
    arrays, args = {}, []
    for name, value in lay.items():
        arrays[name + "_dram"] = np.ascontiguousarray(value)
        args.append(nc.dram_tensor(name + "_dram", value.shape, F32, kind="ExternalInput").ap())
    args.append(nc.dram_tensor("out_dram", (P, TILES, DM), F32, kind="ExternalOutput").ap())
    build(nc, *args)
    r = run_bass_kernel_spmd(nc, [arrays], core_ids=[0])
    got = r.results[0]["out_dram"]
    return np.ascontiguousarray(got.transpose(1, 0, 2)).reshape(BATCH, SEQ, DM)
```

```python
from contextlib import ExitStack

import concourse.bass as bass
from concourse import mybir

F32 = mybir.dt.float32
F32R = mybir.dt.float32r
ALU = mybir.AluOpType
ACT = mybir.ActivationFunctionType
AX = mybir.AxisListType

P = 128
BATCH, SEQ, DM = 4, 256, 256
HEADS, HD, WINDOW = 16, 128, 64
CTX = 128
EXPERTS, RANK = 8, 16
LORA_ALPHA = 16.0
EPS = 1e-5
SCALE = float(HD) ** -0.5

TOK = BATCH * SEQ
KT = DM // P
TILES = TOK // P
GROUPS = HEADS // 2
SLOTS = 4
HALVES = BATCH // 2
PASS = GROUPS * 2 // SLOTS
UNITS = HALVES * PASS * SLOTS
LAST_IT = HALVES * PASS - 1
PAIR = 2 * SEQ
S0 = SEQ // 2
S1 = SEQ - WINDOW
SW = S0 + S1
FW = DM + EXPERTS + EXPERTS * RANK
PIECE = 512
QK_H0, QK_H1, WV, WO = range(4)
LOADED = 16


def build(nc, x_nat, x_T, ctx_T, w_qk, w_v, w_o, xq_T, xk_T, x_bias, ffn_T, lora_bT,
          rope_cos, rope_sin, score_mask, identity, below, out):
    ctx = ExitStack()
    with ctx:
        def sb(name, shape, dt=F32):
            return ctx.enter_context(nc.sbuf_tensor(name, shape, dt))

        def bank(name):
            return ctx.enter_context(nc.psum_tensor(name, [P, 512], F32))

        def sem(name):
            return ctx.enter_context(nc.semaphore(name))

        x_hi = sb("x_hi", [P, KT, TOK], F32R)
        x_lo = sb("x_lo", [P, KT, TOK], F32R)
        acc = sb("acc", [P, TILES, DM])
        stage = sb("stage", [P, 4, PIECE])
        ff_sb = sb("ff_sb", [P, 2, 2, FW])
        lora = sb("lora", [P, 2, 2, PAIR // 2])
        qk_hi = sb("qk_hi", [P, 2, 2, KT, HD], F32R)
        qk_lo = sb("qk_lo", [P, 2, 2, KT, HD], F32R)
        v_hi = sb("v_hi", [P, KT, HEADS * HD], F32R)
        v_lo = sb("v_lo", [P, KT, HEADS * HD], F32R)
        o_hi = sb("o_hi", [P, HEADS * DM], F32R)
        o_lo = sb("o_lo", [P, HEADS * DM], F32R)
        rope = sb("rope", [P, 4, PAIR])
        qr = sb("qr", [P, 2, PAIR])
        kr = sb("kr", [P, 2, PAIR])
        masked = sb("masked", [P, 2, SW])
        probs = sb("probs", [P, 2, S0 + SEQ])
        probs_T = sb("probs_T", [P, 2, SW])
        vals = sb("vals", [P, 2, 2, 2, 2 * HD])
        head_hi = sb("head_hi", [P, SLOTS, PAIR], F32R)
        head_lo = sb("head_lo", [P, SLOTS, PAIR], F32R)
        energy = sb("energy", [P, BATCH, 2, SEQ])
        mix_T = sb("mix_T", [P, BATCH, 2, SEQ])
        cosT = sb("cosT", [P, PAIR])
        sinT = sb("sinT", [P, PAIR])
        mask = sb("mask", [P, SW])
        ident = sb("ident", [P, P])
        xq_w = sb("xq_w", [P, CTX])
        xk_w = sb("xk_w", [P, CTX])
        xbias = sb("xbias", [P, 2])
        ffn_w = sb("ffn_w", [P, KT, FW])
        lora_b = sb("lora_b", [P, DM])
        tri = sb("tri", [P, EXPERTS * EXPERTS])
        nmin = sb("nmin", [P, 2, 2])
        carrier = sb("carrier", [1, 2 * SLOTS])
        rsum = sb("rsum", [P, 2, 2])
        rinv = sb("rinv", [P, 2, 2])
        xmax = sb("xmax", [P, BATCH, 2])
        xsum = sb("xsum", [P, BATCH, 2])
        xinv = sb("xinv", [P, BATCH, 2])
        stats = sb("stats", [P, TILES, 6])
        moments = sb("moments", [P, 3, TILES, 2])
        veps = sb("veps", [P, 3, TILES])
        rstd = sb("rstd", [P, 3, TILES])
        power = sb("power", [P, 2])
        nlmax = sb("nlmax", [P, TILES])
        lexp = sb("lexp", [P, TILES, EXPERTS])
        above = sb("above", [P, TILES, EXPERTS * EXPERTS])
        equal = sb("equal", [P, TILES, EXPERTS * EXPERTS])
        rank = sb("rank", [P, TILES * EXPERTS])
        chosen = sb("chosen", [P, TILES, EXPERTS])
        gsum = sb("gsum", [P, TILES])
        ginv = sb("ginv", [P, TILES])
        gate = sb("gate", [P, TILES, EXPERTS])

        x_first = rope[:, 0:2, :]
        x_second = energy[:, 0:2, :, :].rearrange("p a b n -> p a (b n)")
        ctx_sb = kr[:, :, :].rearrange("p a n -> p (a n)")
        flat_vals = vals[:, :, :, :, :].rearrange("p a b c n -> p (a b c n)")
        xq_sb, xk_sb = flat_vals[:, 0:TOK], flat_vals[:, TOK:2 * TOK]

        def x1_T(part):
            i, n = part
            return energy[:, i // 2 % 2, :, i % 2 * P:(i % 2 + n) * P]

        def x2_T(part):
            i, n = part
            return energy[:, 2 + i // 2 % 2, :, i % 2 * P:(i % 2 + n) * P]

        def ff(part):
            i, n = part
            return ff_sb[:, i // 2 % 2, i % 2:i % 2 + n, :]

        def lora_t(part):
            i, n = part
            return lora[:, 0, i // 2 % 2, i % 2 * P:(i % 2 + n) * P].rearrange("p (m n) -> p m n", n=P)

        def lora_tT(part):
            i, n = part
            return lora[:, 1, i // 2 % 2, i % 2 * P:(i % 2 + n) * P]

        def rows(part):
            i, n = part
            return acc[:, i:i + n, :]

        def end(part):
            return part[0] + part[1]

        bank_q, bank_k, bank_vy, bank_o = bank("bank_q"), bank("bank_k"), bank("bank_vy"), bank("bank_o")
        bank_s = [bank("bank_s0"), bank("bank_s1")]
        bank_t = [bank("bank_t0"), bank("bank_t1")]
        proj_bank = bank_s + bank_t
        last_banks = [bank_o, bank_s[0], bank_s[1], bank_vy]
        last_banks_T = [bank_t[0], bank_t[1], bank_q, bank_k]
        bank_y = dict(zip(range(4, TILES), last_banks))
        bank_x1T = {0: bank_t[1], 2: bank_t[1]} | dict(zip(range(4, TILES), last_banks_T))
        bank_xm = {0: bank_q, 2: bank_q} | bank_y
        bank_x2T = {0: bank_t[0], 2: bank_k} | dict(zip(range(4, TILES), last_banks_T))
        bank_ff = {0: bank_s, 2: bank_s} | {i: [b] for i, b in bank_y.items()}
        bank_lT = {0: bank_t[0], 2: bank_k} | dict(zip(range(4, TILES), last_banks_T))
        bank_f = {0: bank_q, 2: bank_q} | bank_y

        ctx_in, xT_in, tab_in, ffn_in = (sem(n) for n in ("ctx_in", "xT_in", "tab_in", "ffn_in"))
        piece_in = [sem(f"piece_in{i}") for i in range(4)]
        hi_done = [sem(f"hi_done{i}") for i in range(4)]
        lo_done = [sem(f"lo_done{i}") for i in range(4)]
        xhi_done, x_split = sem("xhi_done"), sem("x_split")
        xT2_in = sem("xT2_in")
        zeroed = sem("zeroed")
        xproj_ready, xproj_copied = sem("xproj_ready"), sem("xproj_copied")
        energy_ready, xmax_done, xexp_done, xinv_done, energy_done = (
            sem(n) for n in ("energy_ready", "xmax_done", "xexp_done", "xinv_done", "energy_done"))
        mix_ready, mix_copied = sem("mix_ready"), sem("mix_copied")
        q_ready, k_ready, v_ready, v_copied = (sem(n) for n in ("q_ready", "k_ready", "v_ready", "v_copied"))
        q_scaled, k_scaled, q_rotated, k_rotated = (
            sem(n) for n in ("q_scaled", "k_scaled", "q_rotated", "k_rotated"))
        scores_ready, masked_done, exp_done, rinv_done, probs_done = (
            sem(n) for n in ("scores_ready", "masked_done", "exp_done", "rinv_done", "probs_done"))
        t_ready, t_copied, o_ready = sem("t_ready"), sem("t_copied"), sem("o_ready")
        head_hi_done, head_done = sem("head_hi_done"), sem("head_done")
        last_y_ready, last_y_added = sem("last_y_ready"), sem("last_y_added")
        y_ready, y_added = sem("y_ready"), sem("y_added")
        ln_moments = [sem(f"ln_moments{i}") for i in range(3)]
        ln_stats, ln_veps = sem("ln_stats"), sem("ln_veps")
        ln_rstd = [sem(f"ln_rstd{i}") for i in range(3)]
        x1_done, x1T_ready, x1T_copied = sem("x1_done"), sem("x1T_ready"), sem("x1T_copied")
        xm_ready, x2_summed, x2_done, x2T_ready, x2T_copied = (
            sem(n) for n in ("xm_ready", "x2_summed", "x2_done", "x2T_ready", "x2T_copied"))
        ff_ready, ff_copied, base_done, lmax_done, lexp_done, gate_step, lora_done = (
            sem(n) for n in ("ff_ready", "ff_copied", "base_done", "lmax_done", "lexp_done", "gate_step",
                             "lora_done"))
        lT_ready, lT_copied, f_ready, x3_summed, x3_done = (
            sem(n) for n in ("lT_ready", "lT_copied", "f_ready", "x3_summed", "x3_done"))
        out_done = sem("out_done")

        loop_half = [0]

        def back(it, slot, n):
            turns, slot = divmod(slot - n, SLOTS)
            return (it + turns if turns else it), slot

        def present(it, slot, n):
            return not isinstance(it, int) or 0 <= SLOTS * it + slot - n < UNITS

        def first(it):
            return isinstance(it, int) and it == 0

        def half_of(it):
            return it // PASS if isinstance(it, int) else loop_half[0]

        def group_of(it, slot):
            return it * 2 + (slot // 2 - GROUPS * half_of(it))

        def wait(eng, semaphore, it, slot, each, plus):
            value = it * (each * SLOTS) + (each * slot + plus)
            if not isinstance(value, int) or value > 0:
                eng.wait_ge(semaphore, value)

        def wait_piece(eng, semaphore, it, slot, each=1):
            eng.wait_ge(semaphore, it * (2 * each) + each * (slot // 2 + 1))

        def all_steps(eng, step):
            for slot in range(SLOTS):
                step(0, slot)
            loop_half[0] = 0
            with eng.Fori(1, PASS) as it:
                for slot in range(SLOTS):
                    step(it, slot)
            for slot in range(SLOTS):
                step(PASS, slot)
            loop_half[0] = 1
            with eng.Fori(PASS + 1, 2 * PASS - 1) as it:
                for slot in range(SLOTS):
                    step(it, slot)
            for slot in range(SLOTS):
                step(LAST_IT, slot)

        B0, B1 = (0, 2), (2, 2)
        T4, T5, T6, T7 = ((i, 1) for i in range(4, TILES))

        def last(it, slot, n):
            return isinstance(it, int) and it == LAST_IT and slot == n

        def staged(piece):
            if piece == WV:
                return stage[:, piece, :].rearrange("p (k n) -> p k n", k=KT)
            return stage[:, piece, :]

        def weight_part(piece, it, slot, part):
            if piece == WV:
                return (v_hi, v_lo)[part][:, :, bass.ds(group_of(it, slot) * (2 * HD), 2 * HD)]
            if piece == WO:
                return (o_hi, o_lo)[part][:, bass.ds(group_of(it, slot) * (2 * DM), 2 * DM)]
            return (qk_hi, qk_lo)[part][:, piece, :, :, :].rearrange("p a k n -> p (a k n)")

        block = ctx.enter_context(nc.Block())

        @block.sync
        def _(sp):
            def load(piece, n, g):
                src = (w_qk[g, :, 0:PIECE], w_qk[g, :, PIECE:2 * PIECE], w_v[g, :, :], w_o[g, :, :])[piece]
                if not isinstance(n, int) or n:
                    sp.wait_ge(lo_done[piece], n)
                sp.dma_start(stage[:, piece, :], src).then_inc(piece_in[piece], 16)

            sp.dma_start(ctx_sb, ctx_T).then_inc(ctx_in, 16)
            sp.dma_start(xq_w[:, :], xq_T).then_inc(ctx_in, 16)
            sp.dma_start(xk_w[:, :], xk_T).then_inc(ctx_in, 16)
            sp.dma_start(xbias[:, :], x_bias).then_inc(ctx_in, 16)
            sp.dma_start(x_first, x_T[:, :, 0:PAIR]).then_inc(xT_in, 16)
            load(QK_H0, 0, 0)
            sp.dma_start(cosT[:, :], rope_cos).then_inc(tab_in, 16)
            sp.dma_start(sinT[:, :], rope_sin).then_inc(tab_in, 16)
            load(QK_H1, 0, 0)
            load(WV, 0, 0)
            sp.dma_start(mask[:, :], score_mask).then_inc(tab_in, 16)
            sp.dma_start(ident[:, :], identity).then_inc(tab_in, 16)
            load(WO, 0, 0)
            sp.dma_start(acc[:, :, :], x_nat).then_inc(y_added, LOADED)
            sp.dma_start(ffn_w[:, :, :], ffn_T).then_inc(ffn_in, 16)
            sp.dma_start(lora_b[:, :], lora_bT).then_inc(ffn_in, 16)
            sp.dma_start(tri[:, :], below).then_inc(ffn_in, 16)
            load(QK_H0, 1, 1)
            sp.wait_ge(mix_ready, BATCH)
            sp.dma_start(x_second, x_T[:, :, PAIR:2 * PAIR]).then_inc(xT2_in, 16)
            with sp.Fori(1, GROUPS - 1) as n:
                load(QK_H1, n, n)
                load(WV, n, n)
                load(QK_H0, n + 1, n + 1)
                load(WO, n, n)
            load(QK_H1, GROUPS - 1, GROUPS - 1)
            load(WV, GROUPS - 1, GROUPS - 1)
            load(QK_H0, GROUPS, 0)
            load(WO, GROUPS - 1, GROUPS - 1)
            with sp.Fori(0, GROUPS - 1) as g:
                load(QK_H1, g + GROUPS, g)
                load(QK_H0, g + (GROUPS + 1), g + 1)
            load(QK_H1, 2 * GROUPS - 1, GROUPS - 1)
            for part in (B0, B1, T4, T5, T6, T7):
                sp.wait_ge(x3_done, end(part))
                sp.dma_start(out[:, part[0]:end(part), :], rows(part)).then_inc(out_done, 16)
            sp.wait_ge(out_done, 16 * 6)

        @block.tensor
        def _(pe):
            def three_passes(dst, w, x, first, last):
                for n, (a, b) in enumerate(((0, 0), (0, 1), (1, 0))):
                    mm = pe.matmul(dst, w[a], x[b], start=first and n == 0, stop=last and n == 2)
                return mm

            def project(dst, what, it, slot):
                pair, j = half_of(it), slot % 2
                for k in range(KT):
                    mm = three_passes(dst[:, :], (qk_hi[:, j, what, k, :], qk_lo[:, j, what, k, :]),
                                      (x_hi[:, k, pair * PAIR:(pair + 1) * PAIR],
                                       x_lo[:, k, pair * PAIR:(pair + 1) * PAIR]), k == 0, k == KT - 1)
                return mm

            def q_project(it, slot):
                wait_piece(pe, lo_done[slot % 2], it, slot)
                wait(pe, q_scaled, it, slot, 1, 0)
                project(bank_q, 0, it, slot).then_inc(q_ready, 1)

            def k_project(it, slot):
                wait(pe, k_scaled, it, slot, 1, 0)
                project(bank_k, 1, it, slot).then_inc(k_ready, 1)

            def v_project(it, slot):
                if half_of(it) == 0:
                    wait_piece(pe, lo_done[WV], it, slot)
                if first(it):
                    wait(pe, v_copied, it, slot, 1, 0)
                else:
                    wait(pe, y_added, it, slot, 1, LOADED - 3)
                for m in range(2):
                    tok = half_of(it) * PAIR + (slot % 2) * SEQ + m * P
                    for k in range(KT):
                        rhs = [v[:, k, bass.ds(group_of(it, slot) * (2 * HD), 2 * HD)] for v in (v_hi, v_lo)]
                        mm = three_passes(bank_vy[:, m * 2 * HD:(m + 1) * 2 * HD],
                                          (x_hi[:, k, tok:tok + P], x_lo[:, k, tok:tok + P]),
                                          rhs, k == 0, k == KT - 1)
                mm.then_inc(v_ready, 1)

            def scores(it, slot):
                wait(pe, q_rotated, it, slot, 1, 1)
                wait(pe, k_rotated, it, slot, 1, 1)
                q, k = qr[:, slot % 2, :], kr[:, slot % 2, :]
                for b in range(2):
                    wait(pe, masked_done, it, slot, 2, b - 1)
                    o = b * SEQ
                    pe.matmul(bank_s[b][:, 0:S0], q[:, o:o + P], k[:, o:o + P], start=True, stop=True)
                    pe.matmul(bank_s[b][:, S0:SW], q[:, o + P:o + SEQ], k[:, o + WINDOW:o + SEQ],
                              start=True, stop=True).then_inc(scores_ready, 1)

            def transposes(it, slot):
                for b in range(2):
                    wait(pe, probs_done, it, slot, 2, b + 1)
                    wait(pe, t_copied, it, slot, 2, b - 1)
                    t, p = bank_t[b], probs[:, b, :]
                    pe.transpose(t[:, 0:P], p[:, 0:P], ident[:, :])
                    pe.transpose(t[:, P:P + WINDOW], p[0:WINDOW, P:2 * P], ident[0:WINDOW, 0:WINDOW])
                    pe.transpose(t[:, P + WINDOW:SW], p[:, 2 * P:3 * P], ident[:, :]).then_inc(t_ready, 1)

            def attend(it, slot):
                pair, j = divmod(slot, 2)
                wait(pe, head_done, it, slot, 1, 0)
                for b in range(2):
                    wait(pe, v_copied, it, 2 * pair, 1, b + 1)
                    wait(pe, t_copied, it, slot, 2, b + 1)
                    o = b * SEQ
                    v = vals[:, pair, b, :, j * HD:(j + 1) * HD]
                    pe.matmul(bank_o[:, o:o + P + WINDOW], v[:, 0, :], probs_T[:, b, 0:P + WINDOW],
                              start=True, stop=False, skip_group_check=True)
                    pe.matmul(bank_o[:, o + P:o + SEQ], v[:, 1, :], probs_T[:, b, P + WINDOW:SW],
                              start=False, stop=True, skip_group_check=True).then_inc(o_ready, 1)

            def last_out_project(part):
                i = part[0]
                pe.wait_ge(head_done, UNITS)
                c = (i - 4) * P
                for j in range(2):
                    o = ((GROUPS - 1) * 2 + j) * DM
                    mm = three_passes(bank_y[i][:, 0:DM],
                                      (head_hi[:, 2 + j, c:c + P], head_lo[:, 2 + j, c:c + P]),
                                      [w[:, o:o + DM] for w in (o_hi, o_lo)], j == 0, j == 1)
                mm.then_inc(last_y_ready, 1)

            def out_project(it, slot):
                pair, b = divmod(slot, 2)
                if half_of(it) == 0:
                    wait_piece(pe, lo_done[WO], it, slot)
                wait(pe, head_done, it, 2 * pair, 1, 2)
                if present(it, slot, -3):
                    wait(pe, v_copied, *back(it, slot, -3), 1, 1)
                else:
                    wait(pe, y_added, it, slot, 1, LOADED)
                for m in range(2):
                    c = b * SEQ + m * P
                    for j in range(2):
                        rhs = [w[:, bass.ds(group_of(it, slot) * (2 * DM) + j * DM, DM)] for w in (o_hi, o_lo)]
                        mm = three_passes(bank_vy[:, m * DM:(m + 1) * DM],
                                          (head_hi[:, 2 * pair + j, c:c + P], head_lo[:, 2 * pair + j, c:c + P]),
                                          rhs, j == 0, j == 1)
                mm.then_inc(y_ready, 1)

            def step(it, slot):
                if last(it, slot, 2):
                    pe.wait_ge(x2_summed, end(B0))
                q_project(it, slot)
                if last(it, slot, 2):
                    pe.wait_ge(masked_done, 2 * (UNITS - 3))
                    feed_forward(B0)
                k_project(it, slot)
                if first(it) and slot == 0:
                    cross_energy()
                if first(it) and slot == 1:
                    cross_transposes()
                if present(it, slot, 1):
                    v_project(*back(it, slot, 1))
                if last(it, slot, 1):
                    pe.wait_ge(q_scaled, UNITS - 2)
                    cross_mix(B0)
                if last(it, slot, 3):
                    pe.wait_ge(q_scaled, UNITS)
                    lora_add(B0)
                if last(it, slot, 1):
                    pe.wait_ge(x1T_copied, end(B0))
                if last(it, slot, 2):
                    pe.wait_ge(x2T_copied, end(B0))
                if last(it, slot, 3):
                    pe.wait_ge(x1T_copied, end(B1))
                    pe.wait_ge(lT_copied, end(B0))
                if present(it, slot, 2):
                    transposes(*back(it, slot, 2))
                if first(it) and slot == 1:
                    pe.wait_ge(mix_copied, BATCH)
                if last(it, slot, 2):
                    pe.wait_ge(ff_copied, end(B0))
                if present(it, slot, 1):
                    scores(*back(it, slot, 1))
                if present(it, slot, 2):
                    attend(*back(it, slot, 2))
                if present(it, slot, 4):
                    out_project(*back(it, slot, 4))
                if last(it, slot, 0):
                    x1_transposes(B0)
                if last(it, slot, 1):
                    x2_transposes(B0)
                if last(it, slot, 2):
                    x1_transposes(B1)
                    lora_transposes(B0)

            def cross_project():
                pe.wait_ge(ctx_in, 64)
                for n in range(4):
                    w, o = (xq_w, xk_w)[n // 2], (n % 2) * PAIR
                    pe.matmul(proj_bank[n][:, :], w[:, :], ctx_sb[:, o:o + PAIR],
                              start=True, stop=True).then_inc(xproj_ready, 1)

            def cross_energy():
                pe.wait_ge(xproj_copied, 4)
                for b in range(BATCH):
                    for m in range(2):
                        o = b * SEQ
                        mm = pe.matmul(proj_bank[b][:, m * SEQ:(m + 1) * SEQ],
                                       xq_sb[:, o + m * P:o + (m + 1) * P], xk_sb[:, o:o + SEQ],
                                       start=True, stop=True)
                    mm.then_inc(energy_ready, 1)

            def cross_transposes():
                for b in range(BATCH):
                    pe.wait_ge(energy_done, b + 1)
                    for k in range(2):
                        for m in range(2):
                            c = k * SEQ + m * P
                            mm = pe.transpose(proj_bank[b][:, c:c + P], energy[:, b, m, k * P:(k + 1) * P],
                                              ident[:, :])
                    mm.then_inc(mix_ready, 1)

            def transpose_part(part, dst):
                i, n = part
                for k in range(KT):
                    for m in range(n):
                        c = (k * n + m) * P
                        mm = pe.transpose(dst[:, c:c + P], acc[:, i + m, k * P:(k + 1) * P], ident[:, :])
                return mm

            def x1_transposes(part):
                pe.wait_ge(x1_done, end(part))
                transpose_part(part, bank_x1T[part[0]]).then_inc(x1T_ready, part[1])

            def cross_mix(part):
                i, n = part
                pe.wait_ge(x1T_copied, end(part))
                for m in range(n):
                    for k in range(KT):
                        mm = pe.matmul(bank_xm[i][:, m * SEQ:(m + 1) * SEQ], x1_T(part)[:, k, m * P:(m + 1) * P],
                                       mix_T[:, i // 2, k, :], start=(k == 0), stop=(k == KT - 1))
                mm.then_inc(xm_ready, n)

            def x2_transposes(part):
                pe.wait_ge(x2_done, end(part))
                transpose_part(part, bank_x2T[part[0]]).then_inc(x2T_ready, part[1])

            def feed_forward(part):
                i, n = part
                pe.wait_ge(x2T_copied, end(part))
                if part == B0:
                    pe.wait_ge(ffn_in, 48)
                for m in range(n):
                    for k in range(KT):
                        mm = pe.matmul(bank_ff[i][m][:, 0:FW], x2_T(part)[:, k, m * P:(m + 1) * P],
                                       ffn_w[:, k, :], start=(k == 0), stop=(k == KT - 1))
                    mm.then_inc(ff_ready, 1)

            def lora_transposes(part):
                i, n = part
                pe.wait_ge(lora_done, end(part))
                for m in range(n):
                    mm = pe.transpose(bank_lT[i][:, m * P:(m + 1) * P], lora_t(part)[:, m, :], ident[:, :])
                mm.then_inc(lT_ready, n)

            def lora_add(part):
                i, n = part
                pe.wait_ge(lT_copied, end(part))
                for m in range(n):
                    mm = pe.matmul(bank_f[i][:, m * DM:(m + 1) * DM], lora_tT(part)[:, m * P:(m + 1) * P],
                                   lora_b[:, :], start=True, stop=True)
                mm.then_inc(f_ready, n)

            cross_project()
            pe.wait_ge(x_split, 1)
            pe.wait_ge(tab_in, 64)
            all_steps(pe, step)

            scores(LAST_IT, 3)
            v_project(LAST_IT, 3)
            pe.wait_ge(x3_summed, end(B0))
            cross_mix(B1)
            transposes(LAST_IT, 2)
            attend(LAST_IT, 2)
            out_project(LAST_IT, 0)
            pe.wait_ge(k_scaled, UNITS)
            x2_transposes(B1)
            transposes(LAST_IT, 3)
            pe.wait_ge(masked_done, 2 * UNITS)
            feed_forward(B1)
            attend(LAST_IT, 3)
            out_project(LAST_IT, 1)
            last_out_project(T4)
            pe.wait_ge(ff_copied, end(B1))
            last_out_project(T5)
            lora_transposes(B1)
            last_out_project(T6)
            pe.wait_ge(y_added, LOADED + UNITS - 2)
            last_out_project(T7)
            lora_add(B1)
            x1_transposes(T4)
            x1_transposes(T5)
            pe.wait_ge(x3_summed, end(B1))
            x1_transposes(T6)
            cross_mix(T4)
            x1_transposes(T7)
            cross_mix(T5)
            cross_mix(T6)
            cross_mix(T7)
            x2_transposes(T4)
            x2_transposes(T5)
            feed_forward(T4)
            x2_transposes(T6)
            feed_forward(T5)
            x2_transposes(T7)
            feed_forward(T6)
            lora_transposes(T4)
            feed_forward(T7)
            lora_add(T4)
            for part in (T5, T6, T7):
                lora_transposes(part)
                lora_add(part)

        @block.vector
        def _(dve):
            def q_scale(it, slot):
                rotate(it, slot, q_ready, q_rotated, bank_q, 0).then_inc(q_scaled, 1)

            def k_scale(it, slot):
                rotate(it, slot, k_ready, k_rotated, bank_k, 2).then_inc(k_scaled, 1)

            def rotate(it, slot, ready, rotated, src, n):
                wait(dve, ready, it, slot, 1, 1)
                wait(dve, rotated, it, slot, 1, 0)
                h = HD // 2
                dve.tensor_tensor(rope[:, n, :], src[:, :], cosT[:, :], ALU.mult)
                dve.tensor_tensor(rope[0:h, n + 1, :], src[h:HD, :], sinT[h:HD, :], ALU.mult)
                return dve.tensor_tensor(rope[h:HD, n + 1, :], src[0:h, :], sinT[0:h, :], ALU.mult)

            def mask_and_max(it, slot):
                for b in range(2):
                    wait(dve, scores_ready, it, slot, 2, b + 1)
                    wait(dve, exp_done, it, slot, 2, b - 1)
                    dve.memset(carrier[0:1, 2 * slot + b:2 * slot + b + 1], 0.0)
                    for t, (a, z) in enumerate(((0, S0), (S0, SW))):
                        last = dve.tensor_tensor_reduce(masked[:, b, a:z], bank_s[b][:, a:z], mask[:, a:z],
                                                        -SCALE, 3e38, ALU.add, ALU.min, nmin[:, b, t:t + 1])
                    last.then_inc(masked_done, 1)

            def normalise(it, slot):
                for b in range(2):
                    wait(dve, exp_done, it, slot, 2, b + 1)
                    dve.reciprocal(rinv[:, b, :], rsum[:, b, :]).then_inc(rinv_done, 1)
                    wait(dve, rinv_done, it, slot, 2, b + 1)
                    dve.tensor_scalar(probs[:, b, 0:S0], probs[:, b, 0:S0], rinv[:, b, 0:1], None, ALU.mult)
                    dve.tensor_scalar(probs[:, b, P + WINDOW:], probs[:, b, P + WINDOW:], rinv[:, b, 1:2],
                                      None, ALU.mult).then_inc(probs_done, 1)

            def head_low(it, slot):
                wait(dve, head_hi_done, it, slot, 1, 1)
                dve.tensor_tensor(head_lo[:, slot, :], bank_o[:, :], head_hi[:, slot, :].bitcast(F32),
                                  ALU.subtract).then_inc(head_done, 1)

            def add_output(it, slot):
                wait(dve, y_ready, it, slot, 1, 1)
                wait(dve, y_added, it, slot, 1, LOADED)
                sums = rows((4 * half_of(it) + 2 * (slot % 2), 2)).rearrange("p m n -> p (m n)")
                dve.tensor_tensor(sums, bank_vy[:, :], sums, ALU.add).then_inc(y_added, 1)

            def cross_max(b):
                dve.wait_ge(energy_ready, b + 1)
                dve.tensor_reduce(xmax[:, b, :], proj_bank[b][:, :].rearrange("p (m n) -> p m n", m=2),
                                  AX.X, ALU.max, negate=True).then_inc(xmax_done, 1)

            def cross_normalise(b):
                dve.wait_ge(xexp_done, b + 1)
                dve.reciprocal(xinv[:, b, :], xsum[:, b, :]).then_inc(xinv_done, 1)
                dve.wait_ge(xinv_done, b + 1)
                for m in range(2):
                    last = dve.tensor_scalar(energy[:, b, m, :], energy[:, b, m, :], xinv[:, b, m:m + 1],
                                             None, ALU.mult)
                last.then_inc(energy_done, 1)

            def split_x(n, src, landed):
                part = slice(n * PAIR, (n + 1) * PAIR)
                dve.wait_ge(landed, 16)
                dve.tensor_copy(x_hi[:, :, part], src).then_inc(xhi_done, 1)
                dve.wait_ge(xhi_done, n + 1)
                dve.tensor_tensor(x_lo[:, :, part], src, x_hi[:, :, part].bitcast(F32),
                                  ALU.subtract).then_inc(x_split, 1)

            def step(it, slot):
                if last(it, slot, 0):
                    norm_sums(0, B0)
                if last(it, slot, 1):
                    norm_sums(0, B1)
                if last(it, slot, 2):
                    norm_apply(0, B1, x1_done)
                q_scale(it, slot)
                k_scale(it, slot)
                if last(it, slot, 0):
                    norm_apply(0, B0, x1_done)
                if first(it) and slot == 0:
                    for b in range(BATCH):
                        cross_max(b)
                    for b in range(BATCH):
                        cross_normalise(b)
                if first(it) and slot == 3:
                    split_x(1, x_second, xT2_in)
                if last(it, slot, 1):
                    ln2_sums(B0)
                if last(it, slot, 2):
                    gating(B0)
                if last(it, slot, 3):
                    ln3_sums(B0)
                if present(it, slot, 1):
                    mask_and_max(*back(it, slot, 1))
                if last(it, slot, 1):
                    norm_apply(1, B0, x2_done)
                if last(it, slot, 3):
                    norm_apply(2, B0, x3_done)
                if present(it, slot, 1):
                    normalise(*back(it, slot, 1))
                if present(it, slot, 4):
                    add_output(*back(it, slot, 4))
                if present(it, slot, 2):
                    head_low(*back(it, slot, 2))

            counted = 0

            def norm_sums(norm, part):
                nonlocal counted
                i, n = part
                for m in range(i, i + n):
                    dve.bn_stats(stats[:, m, :], acc[:, m, :]).then_inc(ln_stats, 1)
                counted += n
                dve.wait_ge(ln_stats, counted)
                for m in range(i, i + n):
                    last = dve.bn_aggr(moments[:, norm, m, :], stats[:, m, :])
                last.then_inc(ln_moments[norm], n)

            def norm_apply(norm, part, done):
                dve.wait_ge(ln_rstd[norm], end(part))
                for m in range(part[0], end(part)):
                    dve.tensor_scalar(acc[:, m, :], acc[:, m, :], moments[:, norm, m, 0:1],
                                      rstd[:, norm, m:m + 1], ALU.subtract, ALU.mult).then_inc(done, 1)

            def ln1_sums(part):
                i = part[0]
                dve.wait_ge(last_y_ready, i - 3)
                dve.wait_ge(y_added, LOADED + UNITS - 2)
                dve.tensor_tensor(acc[:, i, :], bank_y[i][:, 0:DM], acc[:, i, :],
                                  ALU.add).then_inc(last_y_added, 1)
                dve.wait_ge(last_y_added, i - 3)
                norm_sums(0, part)

            def ln2_sums(part):
                i, n = part
                dve.wait_ge(x1_done, end(part))
                dve.wait_ge(xm_ready, end(part))
                dve.tensor_tensor(rows(part), bank_xm[i][:, 0:n * DM].rearrange("p (m n) -> p m n", m=n),
                                  rows(part), ALU.add).then_inc(x2_summed, n)
                dve.wait_ge(x2_summed, end(part))
                norm_sums(1, part)

            gates = 0

            def own(instruction):
                nonlocal gates
                gates += 1
                instruction.then_inc(gate_step, 1)
                dve.wait_ge(gate_step, gates)

            def gating(part):
                (i, n), e8, z = part, EXPERTS, end(part)
                f = ff(part)
                logit = f[:, :, DM:DM + e8]
                dve.wait_ge(ff_copied, z)
                dve.tensor_reduce(nlmax[:, i:z], logit, AX.X, ALU.max, negate=True).then_inc(lmax_done, n)
                gt = above[:, i:z, :].rearrange("p m (e f) -> p m e f", f=e8)
                eq = equal[:, i:z, :].rearrange("p m (e f) -> p m e f", f=e8)
                other = logit.unsqueeze(2).to_broadcast([P, n, e8, e8])
                mine = logit.unsqueeze(3).to_broadcast([P, n, e8, e8])
                dve.tensor_tensor(eq, other, mine, ALU.is_equal)
                own(dve.tensor_tensor(gt, other, mine, ALU.is_gt))
                own(dve.tensor_tensor(equal[:, i:z, :], equal[:, i:z, :],
                                      tri[:, :].unsqueeze(1).to_broadcast([P, n, e8 * e8]), ALU.mult))
                own(dve.tensor_tensor(above[:, i:z, :], above[:, i:z, :], equal[:, i:z, :], ALU.add))
                own(dve.tensor_reduce(rank[:, i * e8:z * e8],
                                      above[:, i:z, :].rearrange("p m (e f) -> p (m e) f", f=e8), AX.X, ALU.add))
                dve.wait_ge(lexp_done, z)
                own(dve.scalar_tensor_tensor(chosen[:, i:z, :].rearrange("p m e -> p (m e)"),
                                             rank[:, i * e8:z * e8], 1.5,
                                             lexp[:, i:z, :].rearrange("p m e -> p (m e)"), ALU.is_lt, ALU.mult))
                own(dve.tensor_reduce(gsum[:, i:z], chosen[:, i:z, :], AX.X, ALU.add))
                own(dve.reciprocal(ginv[:, i:z], gsum[:, i:z]))
                own(dve.scalar_tensor_tensor(gate[:, i:z, :], chosen[:, i:z, :], LORA_ALPHA,
                                             ginv[:, i:z].unsqueeze(2).to_broadcast([P, n, e8]),
                                             ALU.mult, ALU.mult))
                for m in range(n):
                    dve.tensor_tensor(lora_t(part)[:, m, :].rearrange("p (e r) -> p e r", e=e8),
                                      f[:, m, DM + e8:FW].rearrange("p (e r) -> p e r", e=e8),
                                      gate[:, i + m, :].unsqueeze(2).to_broadcast([P, e8, RANK]),
                                      ALU.mult).then_inc(lora_done, 1)

            def ln3_sums(part):
                i, n = part
                dve.wait_ge(base_done, end(part))
                dve.wait_ge(f_ready, end(part))
                dve.tensor_tensor(rows(part), bank_f[i][:, 0:n * DM].rearrange("p (m n) -> p m n", m=n),
                                  rows(part), ALU.add).then_inc(x3_summed, n)
                dve.wait_ge(x3_summed, end(part))
                norm_sums(2, part)

            for b in range(2):
                dve.memset(probs[:, b, P:P + WINDOW], 0.0).then_inc(zeroed, 1)
            dve.memset(power[:, :], -0.5).then_inc(zeroed, 1)
            split_x(0, x_first, xT_in)
            dve.wait_ge(x_split, 1)
            dve.wait_ge(tab_in, 64)
            all_steps(dve, step)

            mask_and_max(LAST_IT, 3)
            normalise(LAST_IT, 3)
            ln2_sums(B1)
            norm_apply(1, B1, x2_done)
            head_low(LAST_IT, 2)
            add_output(LAST_IT, 0)
            head_low(LAST_IT, 3)
            gating(B1)
            add_output(LAST_IT, 1)
            ln1_sums(T4)
            ln1_sums(T5)
            norm_apply(0, T4, x1_done)
            ln1_sums(T6)
            norm_apply(0, T5, x1_done)
            ln3_sums(B1)
            norm_apply(0, T6, x1_done)
            ln1_sums(T7)
            norm_apply(2, B1, x3_done)
            norm_apply(0, T7, x1_done)
            ln2_sums(T4)
            ln2_sums(T5)
            norm_apply(1, T4, x2_done)
            ln2_sums(T6)
            norm_apply(1, T5, x2_done)
            ln2_sums(T7)
            norm_apply(1, T6, x2_done)
            norm_apply(1, T7, x2_done)
            gating(T4)
            gating(T5)
            ln3_sums(T4)
            gating(T6)
            norm_apply(2, T4, x3_done)
            ln3_sums(T5)
            gating(T7)
            norm_apply(2, T5, x3_done)
            ln3_sums(T6)
            ln3_sums(T7)
            norm_apply(2, T6, x3_done)
            norm_apply(2, T7, x3_done)

        @block.scalar
        def _(act):
            def weight_high(piece, it, slot):
                wait_piece(act, piece_in[piece], it, slot, 16)
                if piece in (QK_H0, QK_H1):
                    wait(act, k_ready, it, slot, 1, -1)
                act.activation(weight_part(piece, it, slot, 0), staged(piece), ACT.Copy).then_inc(hi_done[piece], 1)

            def copy_probs(it, slot):
                for b in range(2):
                    wait(act, t_ready, it, slot, 2, b + 1)
                    wait(act, o_ready, it, slot, 2, b - 1)
                    act.activation(probs_T[:, b, :], bank_t[b][:, 0:SW], ACT.Copy).then_inc(t_copied, 1)

            def head_high(it, slot):
                wait(act, o_ready, it, slot, 2, 2)
                if not first(it):
                    wait(act, y_added, it, 2 * (slot // 2), 1, LOADED - 2)
                act.activation(head_hi[:, slot, :], bank_o[:, :], ACT.Copy).then_inc(head_hi_done, 1)

            def exps(it, slot):
                for b in range(2):
                    wait(act, masked_done, it, slot, 2, b + 1)
                    wait(act, t_ready, it, slot, 2, b - 1)
                    act.activation(probs[:, b, 0:S0], masked[:, b, 0:S0], ACT.Exp, bias=nmin[:, b, 0:1],
                                   scale=-1.0, accum_out=rsum[:, b, 0:1])
                    act.activation(probs[:, b, P + WINDOW:], masked[:, b, S0:SW], ACT.Exp, bias=nmin[:, b, 1:2],
                                   scale=-1.0, accum_out=rsum[:, b, 1:2]).then_inc(exp_done, 1)

            def copy_values(it, slot):
                pair, b = divmod(slot, 2)
                wait(act, v_ready, it, slot, 1, 1)
                wait(act, o_ready, it, 2 * pair, 2, -4)
                act.activation(vals[:, pair, b, :, :].rearrange("p m n -> p (m n)"), bank_vy[:, :],
                               ACT.Copy).then_inc(v_copied, 1)

            def step(it, slot):
                if present(it, slot, -1):
                    ahead = back(it, slot, -1)
                    weight_high(ahead[1] % 2, *ahead)
                if half_of(it) == 0:
                    weight_high((WV, WO)[slot % 2], it, slot)
                if first(it) and slot == 0:
                    cross_exps()
                if first(it) and slot == 1:
                    copy_mix()
                if last(it, slot, 2):
                    copy_ff(B0)
                if present(it, slot, 1):
                    copy_values(*back(it, slot, 1))
                if present(it, slot, 2):
                    copy_probs(*back(it, slot, 2))
                if last(it, slot, 2):
                    gate_exps(B0)
                if present(it, slot, 1):
                    exps(*back(it, slot, 1))
                if present(it, slot, 2):
                    head_high(*back(it, slot, 2))
                if last(it, slot, 0):
                    copy_x1T(B0)
                if last(it, slot, 1):
                    copy_x2T(B0)
                if last(it, slot, 2):
                    copy_x1T(B1)
                    copy_loraT(B0)

            def cross_exps():
                for b in range(BATCH):
                    act.wait_ge(xmax_done, b + 1)
                    for m in range(2):
                        last = act.activation(energy[:, b, m, :], proj_bank[b][:, m * SEQ:(m + 1) * SEQ], ACT.Exp,
                                              bias=xmax[:, b, m:m + 1], accum_out=xsum[:, b, m:m + 1])
                    last.then_inc(xexp_done, 1)

            def copy_mix():
                for b in range(BATCH):
                    act.wait_ge(mix_ready, b + 1)
                    act.activation(mix_T[:, b, :, :].rearrange("p k n -> p (k n)"), proj_bank[b][:, :],
                                   ACT.Copy).then_inc(mix_copied, 1)

            for n in range(4):
                act.wait_ge(xproj_ready, n + 1)
                dst, o = (xq_sb, xk_sb)[n // 2], (n % 2) * PAIR
                act.activation(dst[:, o:o + PAIR], proj_bank[n][:, :], ACT.Identity,
                               bias=xbias[:, n // 2:n // 2 + 1]).then_inc(xproj_copied, 1)

            def copy_T(src, dst, part, copied):
                n = part[1] * P
                act.activation(dst, src[:, 0:KT * n].rearrange("p (k n) -> p k n", k=KT),
                               ACT.Copy).then_inc(copied, part[1])

            def copy_x1T(part):
                act.wait_ge(x1T_ready, end(part))
                copy_T(bank_x1T[part[0]], x1_T(part), part, x1T_copied)

            def copy_x2T(part):
                act.wait_ge(x2T_ready, end(part))
                copy_T(bank_x2T[part[0]], x2_T(part), part, x2T_copied)

            def copy_ff(part):
                if part[0] >= 4:
                    act.wait_ge(base_done, end(part) - 4)
                for m in range(part[1]):
                    act.wait_ge(ff_ready, part[0] + m + 1)
                    act.activation(ff(part)[:, m, :], bank_ff[part[0]][m][:, 0:FW],
                                   ACT.Copy).then_inc(ff_copied, 1)

            def gate_exps(part):
                act.wait_ge(lmax_done, end(part))
                for m in range(part[1]):
                    i = part[0] + m
                    act.activation(lexp[:, i, :], ff(part)[:, m, DM:DM + EXPERTS], ACT.Exp,
                                   bias=nlmax[:, i:i + 1]).then_inc(lexp_done, 1)

            def copy_loraT(part):
                act.wait_ge(lT_ready, end(part))
                act.activation(lora_tT(part), bank_lT[part[0]][:, 0:part[1] * P],
                               ACT.Copy).then_inc(lT_copied, part[1])

            weight_high(QK_H0, 0, 0)
            act.wait_ge(zeroed, 3)
            all_steps(act, step)

            exps(LAST_IT, 3)
            copy_values(LAST_IT, 3)
            copy_probs(LAST_IT, 2)
            head_high(LAST_IT, 2)
            copy_x2T(B1)
            copy_probs(LAST_IT, 3)
            copy_ff(B1)
            head_high(LAST_IT, 3)
            gate_exps(B1)
            copy_loraT(B1)
            for part in (T4, T5, T6, T7):
                copy_x1T(part)
            copy_x2T(T4)
            copy_x2T(T5)
            copy_ff(T4)
            copy_x2T(T6)
            copy_ff(T5)
            copy_x2T(T7)
            gate_exps(T4)
            copy_ff(T6)
            gate_exps(T5)
            copy_loraT(T4)
            copy_ff(T7)
            gate_exps(T6)
            copy_loraT(T5)
            gate_exps(T7)
            copy_loraT(T6)
            copy_loraT(T7)

        @block.gpsimd
        def _(pool):
            def weight_low(piece, it, slot):
                wait_piece(pool, hi_done[piece], it, slot)
                pool.tensor_tensor(weight_part(piece, it, slot, 1), staged(piece),
                                   weight_part(piece, it, slot, 0).bitcast(F32),
                                   ALU.subtract).then_inc(lo_done[piece], 1)

            def rotate(it, slot, scaled, n, dst, rotated):
                wait(pool, scaled, it, slot, 1, 1)
                wait(pool, scores_ready, it, slot, 2, -2)
                pool.tensor_tensor(dst[:, slot % 2, :], rope[:, n, :], rope[:, n + 1, :],
                                   ALU.add).then_inc(rotated, 1)

            def step(it, slot):
                if present(it, slot, -1):
                    ahead = back(it, slot, -1)
                    weight_low(ahead[1] % 2, *ahead)
                if half_of(it) == 0:
                    weight_low((WV, WO)[slot % 2], it, slot)
                if last(it, slot, 0):
                    inverse_std(0, B0)
                if last(it, slot, 1):
                    inverse_std(0, B1)
                rotate(it, slot, q_scaled, 0, qr, q_rotated)
                rotate(it, slot, k_scaled, 2, kr, k_rotated)
                if last(it, slot, 1):
                    inverse_std(1, B0)
                if last(it, slot, 2):
                    add_dense(B0)
                if last(it, slot, 3):
                    inverse_std(2, B0)

            count = 0

            def inverse_std(norm, part):
                nonlocal count
                i, z = part[0], end(part)
                pool.wait_ge(ln_moments[norm], z)
                pool.tensor_scalar(veps[:, norm, i:z], moments[:, norm, i:z, 1], EPS, None,
                                   ALU.add).then_inc(ln_veps, 1)
                count += 1
                pool.wait_ge(ln_veps, count)
                pool.tensor_tensor(rstd[:, norm, i:z], veps[:, norm, i:z], power[:, 0:z - i],
                                   ALU.pow).then_inc(ln_rstd[norm], z - i)

            def add_dense(part):
                pool.wait_ge(ff_copied, end(part))
                pool.tensor_tensor(rows(part), rows(part), ff(part)[:, :, 0:DM],
                                   ALU.add).then_inc(base_done, part[1])

            pool.wait_ge(zeroed, 3)
            weight_low(QK_H0, 0, 0)
            all_steps(pool, step)

            inverse_std(1, B1)
            add_dense(B1)
            for part in (T4, T5, T6):
                inverse_std(0, part)
            inverse_std(2, B1)
            inverse_std(0, T7)
            for part in (T4, T5, T6, T7):
                inverse_std(1, part)
            for part in (T4, T5, T6, T7):
                add_dense(part)
            for part in (T4, T5, T6, T7):
                inverse_std(2, part)


def kernel(**inputs):
    import numpy as np
    import concourse.bacc as bacc
    from concourse.bass_utils import run_bass_kernel_spmd

    f32 = np.float32
    a = {k: np.asarray(v) for k, v in inputs.items()}
    x = a["x"].reshape(TOK, DM)
    wqkv, inner = a["L0_attn_w_qkv"], HEADS * HD

    qk = wqkv[:2 * inner].reshape(2, GROUPS, 2, HD, KT, P)
    v = wqkv[2 * inner:].reshape(GROUPS, 2 * HD, KT, P)
    o = a["L0_attn_w_o"].reshape(DM, GROUPS, 2, HD)
    lay = {
        "x_nat": x.reshape(TILES, P, DM).transpose(1, 0, 2),
        "x_T": x.reshape(TOK, KT, P).transpose(2, 1, 0),
        "ctx_T": a["ctx_1024"].reshape(TOK, CTX).T,
        "w_qk": qk.transpose(1, 5, 2, 0, 4, 3).reshape(GROUPS, P, 2 * PIECE),
        "w_v": v.transpose(0, 3, 2, 1).reshape(GROUPS, P, PIECE),
        "w_o": o.transpose(1, 3, 2, 0).reshape(GROUPS, P, PIECE),
        "xq_T": a["L0_xattn_Wq"].T,
        "xk_T": a["L0_xattn_Wk"].T,
        "x_bias": np.stack([a["L0_xattn_bq"], a["L0_xattn_bk"]], axis=1),
        "ffn_T": np.concatenate([a["L0_ffn_weight"], a["L0_ffn_gate_w"],
                                 a["L0_ffn_A_w"].reshape(EXPERTS * RANK, DM)], axis=0)
                   .reshape(FW, KT, P).transpose(2, 1, 0),
        "lora_bT": a["L0_ffn_B_w"].transpose(0, 2, 1).reshape(EXPERTS * RANK, DM),
    }

    half = HD // 2
    inv_freq = (f32(1.0) / f32(10000.0) ** (np.arange(0, HD, 2, dtype=f32) / f32(HD))).astype(f32)
    angle = inv_freq[:, None] * np.arange(SEQ, dtype=f32)[None, :]
    cos, sin = np.cos(angle).astype(f32), np.sin(angle).astype(f32)
    query = np.arange(P)[:, None]
    key0, key1 = np.arange(S0)[None, :], np.arange(WINDOW, SEQ)[None, :]
    seen = np.concatenate([(key0 <= query) & (key0 > query - WINDOW),
                           (key1 <= query + P) & (key1 > query + P - WINDOW)], axis=1)
    expert = np.arange(EXPERTS)
    lay |= {
        "rope_cos": np.tile(np.concatenate([cos, cos]), (1, 2)),
        "rope_sin": np.tile(np.concatenate([sin, -sin]), (1, 2)),
        "score_mask": np.where(seen, f32(0), f32(-1e30)),
        "identity": np.eye(P, dtype=f32),
        "below": np.tile((expert[None, :] < expert[:, None]).astype(f32).reshape(1, -1), (P, 1)),
    }

    nc = bacc.Bacc("TRN2", target_bir_lowering=False, num_devices=1)
    arrays, args = {}, []
    for name, value in lay.items():
        arrays[name + "_dram"] = np.ascontiguousarray(value)
        args.append(nc.dram_tensor(name + "_dram", value.shape, F32, kind="ExternalInput").ap())
    args.append(nc.dram_tensor("out_dram", (P, TILES, DM), F32, kind="ExternalOutput").ap())
    build(nc, *args)
    r = run_bass_kernel_spmd(nc, [arrays], core_ids=[0])
    got = r.results[0]["out_dram"]
    return np.ascontiguousarray(got.transpose(1, 0, 2)).reshape(BATCH, SEQ, DM)
```

```python
from contextlib import ExitStack

import concourse.bass as bass
from concourse import mybir

F32 = mybir.dt.float32
F32R = mybir.dt.float32r
ALU = mybir.AluOpType
ACT = mybir.ActivationFunctionType
AX = mybir.AxisListType

P = 128
BATCH, SEQ, DM = 4, 256, 256
HEADS, HD, WINDOW = 16, 128, 64
CTX = 128
EXPERTS, RANK = 8, 16
LORA_ALPHA = 16.0
EPS = 1e-5
SCALE = float(HD) ** -0.5

TOK = BATCH * SEQ
KT = DM // P
TILES = TOK // P
GROUPS = HEADS // 2
SLOTS = 4
HALVES = BATCH // 2
PASS = GROUPS * 2 // SLOTS
UNITS = HALVES * PASS * SLOTS
LAST_IT = HALVES * PASS - 1
PAIR = 2 * SEQ
S0 = SEQ // 2
S1 = SEQ - WINDOW
SW = S0 + S1
FW = DM + EXPERTS + EXPERTS * RANK
PIECE = 512
QK_H0, QK_H1, WV, WO = range(4)
LOADED = 16


def build(nc, x_nat, x_T, ctx_T, w_qk, w_v, w_o, cross_wT, ffn_T, lora_bT,
          rope_cos, rope_sin, score_mask, identity, below, out):
    ctx = ExitStack()
    with ctx:
        def sb(name, shape, dt=F32):
            return ctx.enter_context(nc.sbuf_tensor(name, shape, dt))

        def bank(name):
            return ctx.enter_context(nc.psum_tensor(name, [P, 512], F32))

        def sem(name):
            return ctx.enter_context(nc.semaphore(name))

        x_hi = sb("x_hi", [P, KT, TOK], F32R)
        x_lo = sb("x_lo", [P, KT, TOK], F32R)
        acc = sb("acc", [P, TILES, DM])
        stage = sb("stage", [P, 4, PIECE])
        ff_sb = sb("ff_sb", [P, 2, 2, FW])
        lora = sb("lora", [P, 2, 2, PAIR // 2])
        qk_hi = sb("qk_hi", [P, 2, 2, KT, HD], F32R)
        qk_lo = sb("qk_lo", [P, 2, 2, KT, HD], F32R)
        v_hi = sb("v_hi", [P, KT, HEADS * HD], F32R)
        v_lo = sb("v_lo", [P, KT, HEADS * HD], F32R)
        o_hi = sb("o_hi", [P, HEADS * DM], F32R)
        o_lo = sb("o_lo", [P, HEADS * DM], F32R)
        rope = sb("rope", [P, 4, PAIR])
        qr = sb("qr", [P, 2, PAIR])
        kr = sb("kr", [P, 2, PAIR])
        masked = sb("masked", [P, 2, SW])
        probs = sb("probs", [P, 2, S0 + SEQ])
        probs_T = sb("probs_T", [P, 2, SW])
        vals = sb("vals", [P, 2, 2, 2, 2 * HD])
        head_hi = sb("head_hi", [P, SLOTS, PAIR], F32R)
        head_lo = sb("head_lo", [P, SLOTS, PAIR], F32R)
        energy = sb("energy", [P, BATCH, 2, SEQ])
        mix_T = sb("mix_T", [P, BATCH, 2, SEQ])
        cosT = sb("cosT", [P, PAIR])
        sinT = sb("sinT", [P, PAIR])
        mask = sb("mask", [P, SW])
        ident = sb("ident", [P, P])
        cross_w = sb("cross_w", [P, 2 * CTX + 2])
        xq_w, xk_w, xbias = cross_w[:, 0:CTX], cross_w[:, CTX:2 * CTX], cross_w[:, 2 * CTX:]
        ffn_w = sb("ffn_w", [P, KT, FW])
        lora_b = sb("lora_b", [P, DM])
        tri = sb("tri", [P, EXPERTS * EXPERTS])
        nmin = sb("nmin", [P, 2, 2])
        carrier = sb("carrier", [1, 2 * SLOTS])
        rsum = sb("rsum", [P, 2, 2])
        rinv = sb("rinv", [P, 2, 2])
        xmax = sb("xmax", [P, BATCH, 2])
        xsum = sb("xsum", [P, BATCH, 2])
        xinv = sb("xinv", [P, BATCH, 2])
        stats = sb("stats", [P, TILES, 6])
        moments = sb("moments", [P, 3, TILES, 2])
        veps = sb("veps", [P, 3, TILES])
        rstd = sb("rstd", [P, 3, TILES])
        nshift = sb("nshift", [P, 3, TILES])
        power = sb("power", [P, 2])
        nlmax = sb("nlmax", [P, TILES])
        lexp = sb("lexp", [P, TILES, EXPERTS])
        before = sb("before", [P, TILES, EXPERTS, 2, EXPERTS])
        rank = sb("rank", [P, TILES * EXPERTS])
        chosen = sb("chosen", [P, TILES, EXPERTS])
        gsum = sb("gsum", [P, TILES])
        ginv = sb("ginv", [P, TILES])

        x_first = rope[:, 0:2, :]
        x_second = energy[:, 0:2, :, :].rearrange("p a b n -> p a (b n)")
        ctx_sb = kr[:, :, :].rearrange("p a n -> p (a n)")
        flat_vals = vals[:, :, :, :, :].rearrange("p a b c n -> p (a b c n)")
        xq_sb, xk_sb = flat_vals[:, 0:TOK], flat_vals[:, TOK:2 * TOK]

        def x1_T(part):
            i, n = part
            return energy[:, i // 2 % 2, :, i % 2 * P:(i % 2 + n) * P]

        def x2_T(part):
            i, n = part
            return energy[:, 2 + i // 2 % 2, :, i % 2 * P:(i % 2 + n) * P]

        def ff(part):
            i, n = part
            return ff_sb[:, i // 2 % 2, i % 2:i % 2 + n, :]

        def lora_t(part):
            i, n = part
            return lora[:, 0, i // 2 % 2, i % 2 * P:(i % 2 + n) * P].rearrange("p (m n) -> p m n", n=P)

        def lora_tT(part):
            i, n = part
            return lora[:, 1, i // 2 % 2, i % 2 * P:(i % 2 + n) * P]

        def rows(part):
            i, n = part
            return acc[:, i:i + n, :]

        def residual_in_bank(norm, part):
            return part[0] >= 4 and norm >= 1

        def end(part):
            return part[0] + part[1]

        bank_q, bank_k, bank_vy, bank_o = bank("bank_q"), bank("bank_k"), bank("bank_vy"), bank("bank_o")
        bank_s = [bank("bank_s0"), bank("bank_s1")]
        bank_t = [bank("bank_t0"), bank("bank_t1")]
        proj_bank = bank_s + bank_t
        last_banks = [bank_o, bank_s[0], bank_s[1], bank_vy]
        last_banks_T = [bank_t[0], bank_t[1], bank_t[0], bank_t[1]]
        bank_y = dict(zip(range(4, TILES), last_banks))
        bank_x1T = {0: bank_t[1], 2: bank_t[1]} | dict(zip(range(4, TILES), last_banks_T))
        bank_xm = {0: bank_q, 2: bank_q} | bank_y
        bank_x2T = {0: bank_t[0], 2: bank_k} | dict(zip(range(4, TILES), last_banks_T))
        bank_ff = {0: bank_s, 2: [bank_q, bank_k]} | {i: [bank_x2T[i]] for i in range(4, TILES)}
        bank_lT = {0: bank_t[0], 2: bank_k} | dict(zip(range(4, TILES), last_banks_T))
        bank_f = {0: bank_q, 2: bank_q} | bank_y

        ctx_in = [sem(f"ctx_in{i}") for i in range(2)]
        xT_in, tab_in, ffn_in = (sem(n) for n in ("xT_in", "tab_in", "ffn_in"))
        piece_in = [sem(f"piece_in{i}") for i in range(4)]
        hi_done = [sem(f"hi_done{i}") for i in range(4)]
        lo_done = [sem(f"lo_done{i}") for i in range(4)]
        xhi_done, x_split = sem("xhi_done"), sem("x_split")
        xT2_in = sem("xT2_in")
        zeroed = sem("zeroed")
        xproj_ready, xproj_copied = sem("xproj_ready"), sem("xproj_copied")
        energy_ready, xmax_done, xexp_done, xinv_done, energy_done = (
            sem(n) for n in ("energy_ready", "xmax_done", "xexp_done", "xinv_done", "energy_done"))
        mix_ready, mix_copied = sem("mix_ready"), sem("mix_copied")
        q_ready, k_ready, v_ready, v_copied = (sem(n) for n in ("q_ready", "k_ready", "v_ready", "v_copied"))
        q_scaled, k_scaled, q_rotated, k_rotated = (
            sem(n) for n in ("q_scaled", "k_scaled", "q_rotated", "k_rotated"))
        scores_ready, masked_done, exp_done, rinv_done, probs_done = (
            sem(n) for n in ("scores_ready", "masked_done", "exp_done", "rinv_done", "probs_done"))
        t_ready, t_copied, o_ready = sem("t_ready"), sem("t_copied"), sem("o_ready")
        head_hi_done, head_done = sem("head_hi_done"), sem("head_done")
        last_y_ready, last_y_added = sem("last_y_ready"), sem("last_y_added")
        y_ready, y_added = sem("y_ready"), sem("y_added")
        ln_moments = [sem(f"ln_moments{i}") for i in range(3)]
        ln_stats, ln_veps = sem("ln_stats"), sem("ln_veps")
        ln_rstd = [sem(f"ln_rstd{i}") for i in range(3)]
        x1_done, x1T_ready, x1T_copied = sem("x1_done"), sem("x1T_ready"), sem("x1T_copied")
        xm_ready, x2_summed, x2_done, x2T_ready, x2T_copied = (
            sem(n) for n in ("xm_ready", "x2_summed", "x2_done", "x2T_ready", "x2T_copied"))
        shift_done, x3_done_act = sem("shift_done"), sem("x3_done_act")
        ff_ready, ff_copied, base_done, lmax_done, lexp_done, gate_step, lora_done = (
            sem(n) for n in ("ff_ready", "ff_copied", "base_done", "lmax_done", "lexp_done", "gate_step",
                             "lora_done"))
        lT_ready, lT_copied, f_ready, x3_summed, x3_done = (
            sem(n) for n in ("lT_ready", "lT_copied", "f_ready", "x3_summed", "x3_done"))
        out_done = sem("out_done")

        loop_half = [0]

        def back(it, slot, n):
            turns, slot = divmod(slot - n, SLOTS)
            return (it + turns if turns else it), slot

        def present(it, slot, n):
            return not isinstance(it, int) or 0 <= SLOTS * it + slot - n < UNITS

        def first(it):
            return isinstance(it, int) and it == 0

        def half_of(it):
            return it // PASS if isinstance(it, int) else loop_half[0]

        def group_of(it, slot):
            return it * 2 + (slot // 2 - GROUPS * half_of(it))

        def wait(eng, semaphore, it, slot, each, plus):
            value = it * (each * SLOTS) + (each * slot + plus)
            if not isinstance(value, int) or value > 0:
                eng.wait_ge(semaphore, value)

        def wait_piece(eng, semaphore, it, slot, each=1):
            eng.wait_ge(semaphore, it * (2 * each) + each * (slot // 2 + 1))

        def all_steps(eng, step):
            for slot in range(SLOTS):
                step(0, slot)
            loop_half[0] = 0
            with eng.Fori(1, PASS) as it:
                for slot in range(SLOTS):
                    step(it, slot)
            for slot in range(SLOTS):
                step(PASS, slot)
            loop_half[0] = 1
            with eng.Fori(PASS + 1, 2 * PASS - 1) as it:
                for slot in range(SLOTS):
                    step(it, slot)
            for slot in range(SLOTS):
                step(LAST_IT, slot)

        B0, B1 = (0, 2), (2, 2)
        T4, T5, T6, T7 = ((i, 1) for i in range(4, TILES))
        T45, T67 = (4, 2), (6, 2)

        def first_of_second_half(it, slot):
            return isinstance(it, int) and it == PASS and slot == 0

        def last(it, slot, n):
            return isinstance(it, int) and it == LAST_IT and slot == n

        def staged(piece):
            if piece == WV:
                return stage[:, piece, :].rearrange("p (k n) -> p k n", k=KT)
            return stage[:, piece, :]

        def weight_part(piece, it, slot, part):
            if piece == WV:
                return (v_hi, v_lo)[part][:, :, bass.ds(group_of(it, slot) * (2 * HD), 2 * HD)]
            if piece == WO:
                return (o_hi, o_lo)[part][:, bass.ds(group_of(it, slot) * (2 * DM), 2 * DM)]
            return (qk_hi, qk_lo)[part][:, piece, :, :, :].rearrange("p a k n -> p (a k n)")

        block = ctx.enter_context(nc.Block())

        @block.sync
        def _(sp):
            def load(piece, n, g):
                src = (w_qk[g, :, 0:PIECE], w_qk[g, :, PIECE:2 * PIECE], w_v[g, :, :], w_o[g, :, :])[piece]
                if not isinstance(n, int) or n:
                    sp.wait_ge(lo_done[piece], n)
                sp.dma_start(stage[:, piece, :], src).then_inc(piece_in[piece], 16)

            sp.dma_start(ctx_sb[:, 0:PAIR], ctx_T[:, 0:PAIR]).then_inc(ctx_in[0], 16)
            sp.dma_start(cross_w[:, :], cross_wT).then_inc(ctx_in[0], 16)
            sp.dma_start(ctx_sb[:, PAIR:2 * PAIR], ctx_T[:, PAIR:2 * PAIR]).then_inc(ctx_in[1], 16)
            sp.dma_start(x_first, x_T[:, :, 0:PAIR]).then_inc(xT_in, 16)
            load(QK_H0, 0, 0)
            sp.dma_start(cosT[:, :], rope_cos).then_inc(tab_in, 16)
            sp.dma_start(sinT[:, :], rope_sin).then_inc(tab_in, 16)
            load(QK_H1, 0, 0)
            load(WV, 0, 0)
            sp.dma_start(mask[:, :], score_mask).then_inc(tab_in, 16)
            sp.dma_start(ident[:, :], identity).then_inc(tab_in, 16)
            load(WO, 0, 0)
            sp.dma_start(acc[:, :, :], x_nat).then_inc(y_added, LOADED)
            sp.dma_start(ffn_w[:, :, :], ffn_T).then_inc(ffn_in, 16)
            sp.dma_start(lora_b[:, :], lora_bT).then_inc(ffn_in, 16)
            sp.dma_start(tri[:, :], below).then_inc(ffn_in, 16)
            load(QK_H0, 1, 1)
            load(QK_H1, 1, 1)
            load(WV, 1, 1)
            sp.wait_ge(mix_ready, BATCH)
            sp.dma_start(x_second, x_T[:, :, PAIR:2 * PAIR]).then_inc(xT2_in, 16)
            load(QK_H0, 2, 2)
            load(WO, 1, 1)
            with sp.Fori(2, GROUPS - 1) as n:
                load(QK_H1, n, n)
                load(WV, n, n)
                load(QK_H0, n + 1, n + 1)
                load(WO, n, n)
            load(QK_H1, GROUPS - 1, GROUPS - 1)
            load(WV, GROUPS - 1, GROUPS - 1)
            load(QK_H0, GROUPS, 0)
            load(WO, GROUPS - 1, GROUPS - 1)
            with sp.Fori(0, GROUPS - 1) as g:
                load(QK_H1, g + GROUPS, g)
                load(QK_H0, g + (GROUPS + 1), g + 1)
            load(QK_H1, 2 * GROUPS - 1, GROUPS - 1)
            for part, done, count in ((B0, x3_done, 2), (B1, x3_done_act, 2), (T4, x3_done_act, 3),
                                      (T5, x3_done_act, 4), (T6, x3_done, 3), (T7, x3_done, 4)):
                sp.wait_ge(done, count)
                sp.dma_start(out[:, part[0]:end(part), :], rows(part)).then_inc(out_done, 16)
            sp.wait_ge(out_done, 16 * 6)

        @block.tensor
        def _(pe):
            def three_passes(dst, w, x, first, last):
                for n, (a, b) in enumerate(((0, 0), (0, 1), (1, 0))):
                    mm = pe.matmul(dst, w[a], x[b], start=first and n == 0, stop=last and n == 2)
                return mm

            def project(dst, what, it, slot):
                pair, j = half_of(it), slot % 2
                for k in range(KT):
                    mm = three_passes(dst[:, :], (qk_hi[:, j, what, k, :], qk_lo[:, j, what, k, :]),
                                      (x_hi[:, k, pair * PAIR:(pair + 1) * PAIR],
                                       x_lo[:, k, pair * PAIR:(pair + 1) * PAIR]), k == 0, k == KT - 1)
                return mm

            def q_project(it, slot):
                wait_piece(pe, lo_done[slot % 2], it, slot)
                wait(pe, q_scaled, it, slot, 1, 0)
                project(bank_q, 0, it, slot).then_inc(q_ready, 1)

            def k_project(it, slot):
                wait(pe, k_scaled, it, slot, 1, 0)
                project(bank_k, 1, it, slot).then_inc(k_ready, 1)

            def v_project(it, slot):
                if half_of(it) == 0:
                    wait_piece(pe, lo_done[WV], it, slot)
                if first(it):
                    wait(pe, v_copied, it, slot, 1, 0)
                else:
                    wait(pe, y_added, it, slot, 1, LOADED - 3)
                for m in range(2):
                    tok = half_of(it) * PAIR + (slot % 2) * SEQ + m * P
                    for k in range(KT):
                        rhs = [v[:, k, bass.ds(group_of(it, slot) * (2 * HD), 2 * HD)] for v in (v_hi, v_lo)]
                        mm = three_passes(bank_vy[:, m * 2 * HD:(m + 1) * 2 * HD],
                                          (x_hi[:, k, tok:tok + P], x_lo[:, k, tok:tok + P]),
                                          rhs, k == 0, k == KT - 1)
                mm.then_inc(v_ready, 1)

            def scores(it, slot):
                wait(pe, q_rotated, it, slot, 1, 1)
                wait(pe, k_rotated, it, slot, 1, 1)
                q, k = qr[:, slot % 2, :], kr[:, slot % 2, :]
                for b in range(2):
                    wait(pe, masked_done, it, slot, 2, b - 1)
                    o = b * SEQ
                    pe.matmul(bank_s[b][:, 0:S0], q[:, o:o + P], k[:, o:o + P], start=True, stop=True)
                    pe.matmul(bank_s[b][:, S0:SW], q[:, o + P:o + SEQ], k[:, o + WINDOW:o + SEQ],
                              start=True, stop=True).then_inc(scores_ready, 1)

            def transposes(it, slot):
                for b in range(2):
                    wait(pe, probs_done, it, slot, 2, b + 1)
                    wait(pe, t_copied, it, slot, 2, b - 1)
                    t, p = bank_t[b], probs[:, b, :]
                    pe.transpose(t[:, 0:P], p[:, 0:P], ident[:, :])
                    pe.transpose(t[:, P:P + WINDOW], p[0:WINDOW, P:2 * P], ident[0:WINDOW, 0:WINDOW])
                    pe.transpose(t[:, P + WINDOW:SW], p[:, 2 * P:3 * P], ident[:, :]).then_inc(t_ready, 1)

            def attend(it, slot):
                pair, j = divmod(slot, 2)
                wait(pe, head_done, it, slot, 1, 0)
                for b in range(2):
                    wait(pe, v_copied, it, 2 * pair, 1, b + 1)
                    wait(pe, t_copied, it, slot, 2, b + 1)
                    o = b * SEQ
                    v = vals[:, pair, b, :, j * HD:(j + 1) * HD]
                    pe.matmul(bank_o[:, o:o + P + WINDOW], v[:, 0, :], probs_T[:, b, 0:P + WINDOW],
                              start=True, stop=False, skip_group_check=True)
                    pe.matmul(bank_o[:, o + P:o + SEQ], v[:, 1, :], probs_T[:, b, P + WINDOW:SW],
                              start=False, stop=True, skip_group_check=True).then_inc(o_ready, 1)

            def add_residual(part, bank, stop):
                return pe.matmul(bank[:, 0:DM], ident[:, :], acc[:, part[0], :], start=False, stop=stop)

            def last_out_project(part):
                i = part[0]
                pe.wait_ge(head_done, UNITS)
                c = (i - 4) * P
                for j in range(2):
                    o = ((GROUPS - 1) * 2 + j) * DM
                    mm = three_passes(bank_y[i][:, 0:DM],
                                      (head_hi[:, 2 + j, c:c + P], head_lo[:, 2 + j, c:c + P]),
                                      [w[:, o:o + DM] for w in (o_hi, o_lo)], j == 0, j == 1)
                mm.then_inc(last_y_ready, 1)

            def out_project(it, slot):
                pair, b = divmod(slot, 2)
                if half_of(it) == 0:
                    wait_piece(pe, lo_done[WO], it, slot)
                wait(pe, head_done, it, 2 * pair, 1, 2)
                if present(it, slot, -3):
                    wait(pe, v_copied, *back(it, slot, -3), 1, 1)
                else:
                    wait(pe, y_added, it, slot, 1, LOADED)
                for m in range(2):
                    c = b * SEQ + m * P
                    for j in range(2):
                        rhs = [w[:, bass.ds(group_of(it, slot) * (2 * DM) + j * DM, DM)] for w in (o_hi, o_lo)]
                        mm = three_passes(bank_vy[:, m * DM:(m + 1) * DM],
                                          (head_hi[:, 2 * pair + j, c:c + P], head_lo[:, 2 * pair + j, c:c + P]),
                                          rhs, j == 0, j == 1)
                mm.then_inc(y_ready, 1)

            def step(it, slot):
                if last(it, slot, 2):
                    pe.wait_ge(x2_summed, end(B0))
                if first_of_second_half(it, slot):
                    pe.wait_ge(x_split, 2)
                q_project(it, slot)
                k_project(it, slot)
                if last(it, slot, 1):
                    x1_transposes(B0)
                if last(it, slot, 3):
                    x1_transposes(B1)
                    lora_transposes(B0)
                if last(it, slot, 2):
                    x2_transposes(B0)
                if first(it) and slot == 0:
                    cross_energy()
                if first(it) and slot == 1:
                    cross_transposes()
                if present(it, slot, 1):
                    v_project(*back(it, slot, 1))
                if last(it, slot, 2):
                    pe.wait_ge(masked_done, 2 * (UNITS - 3))
                    feed_forward(B0)
                if last(it, slot, 1):
                    pe.wait_ge(x1T_copied, end(B0))
                if last(it, slot, 3):
                    pe.wait_ge(x1T_copied, end(B1))
                    pe.wait_ge(lT_copied, end(B0))
                if present(it, slot, 2):
                    transposes(*back(it, slot, 2))
                if first(it) and slot == 1:
                    pe.wait_ge(mix_copied, BATCH)
                if last(it, slot, 1):
                    pe.wait_ge(q_scaled, UNITS - 2)
                    cross_mix(B0)
                if last(it, slot, 2):
                    pe.wait_ge(ff_copied, end(B0))
                if last(it, slot, 3):
                    pe.wait_ge(q_scaled, UNITS)
                    lora_add(B0)
                if present(it, slot, 1):
                    scores(*back(it, slot, 1))
                if present(it, slot, 2):
                    attend(*back(it, slot, 2))
                if present(it, slot, 4):
                    out_project(*back(it, slot, 4))

            def cross_project():
                for n in range(4):
                    pe.wait_ge(ctx_in[n // 2], (32, 16)[n // 2])
                    w, o = (xq_w, xk_w)[n % 2], (n // 2) * PAIR
                    pe.matmul(proj_bank[n][:, :], w[:, :], ctx_sb[:, o:o + PAIR],
                              start=True, stop=True).then_inc(xproj_ready, 1)

            def cross_energy():
                pe.wait_ge(xproj_copied, 4)
                for b in range(BATCH):
                    for m in range(2):
                        o = b * SEQ
                        mm = pe.matmul(proj_bank[b][:, m * SEQ:(m + 1) * SEQ],
                                       xq_sb[:, o + m * P:o + (m + 1) * P], xk_sb[:, o:o + SEQ],
                                       start=True, stop=True)
                    mm.then_inc(energy_ready, 1)

            def cross_transposes():
                pe.wait_ge(tab_in, 64)
                for b in range(BATCH):
                    pe.wait_ge(energy_done, b + 1)
                    for k in range(2):
                        for m in range(2):
                            c = k * SEQ + m * P
                            mm = pe.transpose(proj_bank[b][:, c:c + P], energy[:, b, m, k * P:(k + 1) * P],
                                              ident[:, :])
                    mm.then_inc(mix_ready, 1)

            def transpose_part(part, dst):
                i, n = part
                for k in range(KT):
                    for m in range(n):
                        c = (k * n + m) * P
                        mm = pe.transpose(dst[:, c:c + P], acc[:, i + m, k * P:(k + 1) * P], ident[:, :])
                return mm

            def x1_transposes(part):
                pe.wait_ge(x1_done, end(part))
                transpose_part(part, bank_x1T[part[0]]).then_inc(x1T_ready, part[1])

            def cross_mix(part):
                i, n = part
                pe.wait_ge(x1T_copied, end(part))
                for m in range(n):
                    for k in range(KT):
                        mm = pe.matmul(bank_xm[i][:, m * SEQ:(m + 1) * SEQ], x1_T(part)[:, k, m * P:(m + 1) * P],
                                       mix_T[:, i // 2, k, :], start=(k == 0),
                                       stop=(k == KT - 1 and not residual_in_bank(1, part)))
                if residual_in_bank(1, part):
                    mm = add_residual(part, bank_xm[i], True)
                mm.then_inc(xm_ready, n)

            def x2_transposes(part):
                pe.wait_ge(x2_done, end(part))
                transpose_part(part, bank_x2T[part[0]]).then_inc(x2T_ready, part[1])

            def feed_forward(part):
                i, n = part
                pe.wait_ge(x2T_copied, end(part))
                if part == B0:
                    pe.wait_ge(ffn_in, 48)
                for m in range(n):
                    for k in range(KT):
                        mm = pe.matmul(bank_ff[i][m][:, 0:FW], x2_T(part)[:, k, m * P:(m + 1) * P],
                                       ffn_w[:, k, :], start=(k == 0), stop=(k == KT - 1))
                    mm.then_inc(ff_ready, 1)

            def last_gates(part):
                pe.wait_ge(x2T_copied, end(part))
                for k in range(KT):
                    mm = pe.matmul(bank_x2T[part[0]][:, DM:FW], x2_T(part)[:, k, :], ffn_w[:, k, DM:FW],
                                   start=(k == 0), stop=(k == KT - 1))
                mm.then_inc(ff_ready, 1)

            def last_dense(part):
                for k in range(KT):
                    pe.matmul(bank_f[part[0]][:, 0:DM], x2_T(part)[:, k, :], ffn_w[:, k, 0:DM],
                              start=(k == 0), stop=False)
                add_residual(part, bank_f[part[0]], False)

            def lora_transposes(part):
                i, n = part
                pe.wait_ge(lora_done, end(part))
                for m in range(n):
                    mm = pe.transpose(bank_lT[i][:, m * P:(m + 1) * P], lora_t(part)[:, m, :], ident[:, :])
                mm.then_inc(lT_ready, n)

            def lora_add(part):
                i, n = part
                pe.wait_ge(lT_copied, end(part))
                for m in range(n):
                    mm = pe.matmul(bank_f[i][:, m * DM:(m + 1) * DM], lora_tT(part)[:, m * P:(m + 1) * P],
                                   lora_b[:, :], start=not residual_in_bank(2, part), stop=True)
                mm.then_inc(f_ready, n)

            cross_project()
            pe.wait_ge(x_split, 1)
            all_steps(pe, step)

            scores(LAST_IT, 3)
            transposes(LAST_IT, 2)
            v_project(LAST_IT, 3)
            pe.wait_ge(x3_summed, end(B0))
            cross_mix(B1)
            attend(LAST_IT, 2)
            transposes(LAST_IT, 3)
            out_project(LAST_IT, 0)
            attend(LAST_IT, 3)
            pe.wait_ge(k_scaled, UNITS)
            x2_transposes(B1)
            out_project(LAST_IT, 1)
            last_out_project(T4)
            pe.wait_ge(masked_done, 2 * UNITS)
            last_out_project(T5)
            last_out_project(T6)
            pe.wait_ge(y_added, LOADED + UNITS - 2)
            last_out_project(T7)
            feed_forward(B1)
            x1_transposes(T4)
            x1_transposes(T5)
            cross_mix(T4)
            x1_transposes(T6)
            cross_mix(T5)
            x1_transposes(T7)
            cross_mix(T6)
            cross_mix(T7)
            lora_transposes(B1)
            x2_transposes(T4)
            lora_add(B1)
            x2_transposes(T5)
            last_gates(T4)
            last_gates(T5)
            last_dense(T4)
            pe.wait_ge(ff_copied, end(T4))
            x2_transposes(T6)
            pe.wait_ge(ff_copied, end(T5))
            x2_transposes(T7)
            last_gates(T6)
            last_gates(T7)
            last_dense(T5)
            pe.wait_ge(ff_copied, end(T6))
            lora_transposes(T4)
            pe.wait_ge(ff_copied, end(T7))
            lora_transposes(T5)
            last_dense(T6)
            lora_add(T4)
            lora_add(T5)
            lora_transposes(T6)
            lora_transposes(T7)
            last_dense(T7)
            lora_add(T6)
            lora_add(T7)

        @block.vector
        def _(dve):
            def q_scale(it, slot):
                rotate(it, slot, q_ready, q_rotated, bank_q, 0).then_inc(q_scaled, 1)

            def k_scale(it, slot):
                rotate(it, slot, k_ready, k_rotated, bank_k, 2).then_inc(k_scaled, 1)

            def rotate(it, slot, ready, rotated, src, n):
                wait(dve, ready, it, slot, 1, 1)
                wait(dve, rotated, it, slot, 1, 0)
                h = HD // 2
                dve.tensor_tensor(rope[:, n, :], src[:, :], cosT[:, :], ALU.mult)
                dve.tensor_tensor(rope[0:h, n + 1, :], src[h:HD, :], sinT[h:HD, :], ALU.mult)
                return dve.tensor_tensor(rope[h:HD, n + 1, :], src[0:h, :], sinT[0:h, :], ALU.mult)

            def mask_and_max(it, slot):
                for b in range(2):
                    wait(dve, scores_ready, it, slot, 2, b + 1)
                    wait(dve, exp_done, it, slot, 2, b - 1)
                    dve.memset(carrier[0:1, 2 * slot + b:2 * slot + b + 1], 0.0)
                    for t, (a, z) in enumerate(((0, S0), (S0, SW))):
                        last = dve.tensor_tensor_reduce(masked[:, b, a:z], bank_s[b][:, a:z], mask[:, a:z],
                                                        -SCALE, 3e38, ALU.add, ALU.min, nmin[:, b, t:t + 1])
                    last.then_inc(masked_done, 1)

            def normalise(it, slot):
                for b in range(2):
                    wait(dve, exp_done, it, slot, 2, b + 1)
                    dve.reciprocal(rinv[:, b, :], rsum[:, b, :]).then_inc(rinv_done, 1)
                    wait(dve, rinv_done, it, slot, 2, b + 1)
                    dve.tensor_scalar(probs[:, b, 0:S0], probs[:, b, 0:S0], rinv[:, b, 0:1], None, ALU.mult)
                    dve.tensor_scalar(probs[:, b, P + WINDOW:], probs[:, b, P + WINDOW:], rinv[:, b, 1:2],
                                      None, ALU.mult).then_inc(probs_done, 1)

            def head_low(it, slot):
                wait(dve, head_hi_done, it, slot, 1, 1)
                dve.tensor_tensor(head_lo[:, slot, :], bank_o[:, :], head_hi[:, slot, :].bitcast(F32),
                                  ALU.subtract).then_inc(head_done, 1)

            def add_output(it, slot):
                wait(dve, y_ready, it, slot, 1, 1)
                wait(dve, y_added, it, slot, 1, LOADED)
                sums = rows((4 * half_of(it) + 2 * (slot % 2), 2)).rearrange("p m n -> p (m n)")
                dve.tensor_tensor(sums, bank_vy[:, :], sums, ALU.add).then_inc(y_added, 1)

            def cross_max(b):
                dve.wait_ge(energy_ready, b + 1)
                dve.tensor_reduce(xmax[:, b, :], proj_bank[b][:, :].rearrange("p (m n) -> p m n", m=2),
                                  AX.X, ALU.max, negate=True).then_inc(xmax_done, 1)

            def cross_normalise(b):
                dve.wait_ge(xexp_done, b + 1)
                dve.reciprocal(xinv[:, b, :], xsum[:, b, :]).then_inc(xinv_done, 1)
                dve.wait_ge(xinv_done, b + 1)
                for m in range(2):
                    last = dve.tensor_scalar(energy[:, b, m, :], energy[:, b, m, :], xinv[:, b, m:m + 1],
                                             None, ALU.mult)
                last.then_inc(energy_done, 1)

            def split_x_first():
                dve.wait_ge(xT_in, 16)
                dve.tensor_copy(x_hi[:, :, 0:PAIR], x_first).then_inc(xhi_done, 1)
                dve.wait_ge(xhi_done, 1)
                dve.tensor_tensor(x_lo[:, :, 0:PAIR], x_first, x_hi[:, :, 0:PAIR].bitcast(F32),
                                  ALU.subtract).then_inc(x_split, 1)

            def step(it, slot):
                q_scale(it, slot)
                k_scale(it, slot)
                if first(it) and slot == 0:
                    for b in range(BATCH):
                        cross_max(b)
                    for b in range(BATCH):
                        cross_normalise(b)
                if present(it, slot, 1):
                    mask_and_max(*back(it, slot, 1))
                if last(it, slot, 0):
                    norm_sums(0, B0)
                    norm_sums(0, B1)
                if last(it, slot, 1):
                    ln2_sums(B0)
                if last(it, slot, 2):
                    gating(B0)
                if last(it, slot, 3):
                    ln3_sums(B0)
                if present(it, slot, 1):
                    normalise(*back(it, slot, 1))
                if last(it, slot, 0):
                    norm_apply(0, B0, x1_done)
                if last(it, slot, 1):
                    norm_apply(1, B0, x2_done)
                if present(it, slot, 4):
                    add_output(*back(it, slot, 4))
                if present(it, slot, 2):
                    head_low(*back(it, slot, 2))
                if last(it, slot, 1):
                    norm_apply(0, B1, x1_done)
                if last(it, slot, 3):
                    norm_apply(2, B0, x3_done)

            counted = 0

            def summed(norm, part, m):
                return bank_y[m][:, 0:DM] if residual_in_bank(norm, part) else acc[:, m, :]

            def norm_sums(norm, part):
                nonlocal counted
                i, n = part
                for m in range(i, i + n):
                    dve.bn_stats(stats[:, m, :], summed(norm, part, m)).then_inc(ln_stats, 1)
                counted += n
                dve.wait_ge(ln_stats, counted)
                for m in range(i, i + n):
                    last = dve.bn_aggr(moments[:, norm, m, :], stats[:, m, :])
                last.then_inc(ln_moments[norm], n)

            def norm_apply(norm, part, done):
                dve.wait_ge(ln_rstd[norm], end(part))
                for m in range(part[0], end(part)):
                    dve.tensor_scalar(acc[:, m, :], summed(norm, part, m), moments[:, norm, m, 0:1],
                                      rstd[:, norm, m:m + 1], ALU.subtract, ALU.mult).then_inc(done, 1)

            def last_ln1_sums(part):
                i = part[0]
                dve.wait_ge(last_y_ready, i - 3)
                dve.wait_ge(y_added, LOADED + UNITS - 2)
                dve.tensor_tensor(acc[:, i, :], bank_y[i][:, 0:DM], acc[:, i, :],
                                  ALU.add).then_inc(last_y_added, 1)
                dve.wait_ge(last_y_added, i - 3)
                norm_sums(0, part)

            def last_sums(norm, part, ready, value):
                dve.wait_ge(ready, value)
                norm_sums(norm, part)

            def ln2_sums(part):
                i, n = part
                dve.wait_ge(x1_done, end(part))
                dve.wait_ge(xm_ready, end(part))
                dve.tensor_tensor(rows(part), bank_xm[i][:, 0:n * DM].rearrange("p (m n) -> p m n", m=n),
                                  rows(part), ALU.add).then_inc(x2_summed, n)
                dve.wait_ge(x2_summed, end(part))
                norm_sums(1, part)

            gates = 0

            def counted_gate(instruction):
                nonlocal gates
                gates += 1
                instruction.then_inc(gate_step, 1)
                return gates

            def gating(part):
                (i, n), e8, z = part, EXPERTS, end(part)
                f = ff(part)
                logit = f[:, :, DM:DM + e8]
                dve.wait_ge(ff_copied, z)
                dve.tensor_reduce(nlmax[:, i:z], logit, AX.X, ALU.max, negate=True).then_inc(lmax_done, n)
                for t in range(i, z):
                    other = logit[:, t - i, :].unsqueeze(1).to_broadcast([P, e8, e8])
                    mine = logit[:, t - i, :].unsqueeze(2).to_broadcast([P, e8, e8])
                    larger, equal = before[:, t, :, 0, :], before[:, t, :, 1, :]
                    compared = counted_gate(dve.tensor_tensor(equal, other, mine, ALU.is_equal))
                    dve.tensor_tensor(larger, other, mine, ALU.is_gt)
                    dve.wait_ge(gate_step, compared)
                    made = counted_gate(dve.tensor_tensor(
                        equal, equal, tri[:, :].rearrange("p (e f) -> p e f", f=e8), ALU.mult))
                dve.wait_ge(gate_step, made)
                made = counted_gate(dve.tensor_reduce(
                    rank[:, i * e8:z * e8], before[:, i:z, :, :, :].rearrange("p m e t f -> p (m e) (t f)"),
                    AX.X, ALU.add))
                dve.wait_ge(lexp_done, z)
                dve.wait_ge(gate_step, made)
                for t in range(i, z):
                    made = counted_gate(dve.scalar_tensor_tensor(
                        chosen[:, t, :], rank[:, t * e8:(t + 1) * e8], 1.5, lexp[:, t, :], ALU.is_lt, ALU.mult,
                        accum_out=gsum[:, t:t + 1]))
                dve.wait_ge(gate_step, made)
                made = counted_gate(dve.reciprocal(ginv[:, i:z], gsum[:, i:z]))
                dve.wait_ge(gate_step, made)
                for t in range(i, z):
                    dve.scalar_tensor_tensor(lora_t(part)[:, t - i, :].rearrange("p (e r) -> p e r", e=e8),
                                             f[:, t - i, DM + e8:FW].rearrange("p (e r) -> p e r", e=e8),
                                             ginv[:, t:t + 1],
                                             chosen[:, t, :].unsqueeze(2).to_broadcast([P, e8, RANK]),
                                             ALU.mult, ALU.mult).then_inc(lora_done, 1)

            def ln3_sums(part):
                i, n = part
                dve.wait_ge(base_done, end(part))
                dve.wait_ge(f_ready, end(part))
                dve.tensor_tensor(rows(part), bank_f[i][:, 0:n * DM].rearrange("p (m n) -> p m n", m=n),
                                  rows(part), ALU.add).then_inc(x3_summed, n)
                dve.wait_ge(x3_summed, end(part))
                norm_sums(2, part)

            for b in range(2):
                dve.memset(probs[:, b, P:P + WINDOW], 0.0).then_inc(zeroed, 1)
            dve.memset(power[:, :], -0.5).then_inc(zeroed, 1)
            split_x_first()
            dve.wait_ge(x_split, 1)
            dve.wait_ge(tab_in, 64)
            all_steps(dve, step)

            mask_and_max(LAST_IT, 3)
            normalise(LAST_IT, 3)
            ln2_sums(B1)
            head_low(LAST_IT, 2)
            norm_apply(1, B1, x2_done)
            add_output(LAST_IT, 0)
            head_low(LAST_IT, 3)
            add_output(LAST_IT, 1)
            last_ln1_sums(T4)
            last_ln1_sums(T5)
            norm_apply(0, T4, x1_done)
            last_ln1_sums(T6)
            norm_apply(0, T5, x1_done)
            last_ln1_sums(T7)
            norm_apply(0, T6, x1_done)
            norm_apply(0, T7, x1_done)
            gating(B1)
            last_sums(1, T4, xm_ready, end(T4))
            norm_apply(1, T4, x2_done)
            last_sums(1, T5, xm_ready, end(T5))
            last_sums(1, T6, xm_ready, end(T6))
            norm_apply(1, T5, x2_done)
            last_sums(1, T7, xm_ready, end(T7))
            norm_apply(1, T6, x2_done)
            norm_apply(1, T7, x2_done)
            ln3_sums(B1)
            gating(T45)
            gating(T67)
            last_sums(2, T4, f_ready, end(T4))
            last_sums(2, T5, f_ready, end(T5))
            last_sums(2, T6, f_ready, end(T6))
            last_sums(2, T7, f_ready, end(T7))
            norm_apply(2, T6, x3_done)
            norm_apply(2, T7, x3_done)

        @block.scalar
        def _(act):
            def weight_high(piece, it, slot):
                wait_piece(act, piece_in[piece], it, slot, 16)
                if piece in (QK_H0, QK_H1):
                    wait(act, k_ready, it, slot, 1, -1)
                act.activation(weight_part(piece, it, slot, 0), staged(piece), ACT.Copy).then_inc(hi_done[piece], 1)

            def copy_probs(it, slot):
                for b in range(2):
                    wait(act, t_ready, it, slot, 2, b + 1)
                    wait(act, o_ready, it, slot, 2, b - 1)
                    act.activation(probs_T[:, b, :], bank_t[b][:, 0:SW], ACT.Copy).then_inc(t_copied, 1)

            def head_high(it, slot):
                wait(act, o_ready, it, slot, 2, 2)
                if not first(it):
                    wait(act, y_added, it, 2 * (slot // 2), 1, LOADED - 2)
                act.activation(head_hi[:, slot, :], bank_o[:, :], ACT.Copy).then_inc(head_hi_done, 1)

            def exps(it, slot):
                for b in range(2):
                    wait(act, masked_done, it, slot, 2, b + 1)
                    wait(act, t_ready, it, slot, 2, b - 1)
                    act.activation(probs[:, b, 0:S0], masked[:, b, 0:S0], ACT.Exp, bias=nmin[:, b, 0:1],
                                   scale=-1.0, accum_out=rsum[:, b, 0:1])
                    act.activation(probs[:, b, P + WINDOW:], masked[:, b, S0:SW], ACT.Exp, bias=nmin[:, b, 1:2],
                                   scale=-1.0, accum_out=rsum[:, b, 1:2]).then_inc(exp_done, 1)

            def copy_values(it, slot):
                pair, b = divmod(slot, 2)
                wait(act, v_ready, it, slot, 1, 1)
                wait(act, o_ready, it, 2 * pair, 2, -4)
                act.activation(vals[:, pair, b, :, :].rearrange("p m n -> p (m n)"), bank_vy[:, :],
                               ACT.Copy).then_inc(v_copied, 1)

            def step(it, slot):
                if present(it, slot, -1):
                    ahead = back(it, slot, -1)
                    weight_high(ahead[1] % 2, *ahead)
                if half_of(it) == 0:
                    weight_high((WV, WO)[slot % 2], it, slot)
                if last(it, slot, 1):
                    copy_x1T(B0)
                if last(it, slot, 3):
                    copy_x1T(B1)
                    copy_loraT(B0)
                if last(it, slot, 2):
                    copy_x2T(B0)
                if first(it) and slot == 2:
                    act.wait_ge(xT2_in, 16)
                    act.activation(x_hi[:, :, PAIR:2 * PAIR], x_second, ACT.Copy).then_inc(xhi_done, 1)
                if first(it) and slot == 0:
                    cross_exps()
                if first(it) and slot == 1:
                    copy_mix()
                if present(it, slot, 1):
                    copy_values(*back(it, slot, 1))
                if last(it, slot, 2):
                    copy_ff(B0)
                if present(it, slot, 2):
                    copy_probs(*back(it, slot, 2))
                if present(it, slot, 1):
                    exps(*back(it, slot, 1))
                if last(it, slot, 2):
                    gate_exps(B0)
                if present(it, slot, 2):
                    head_high(*back(it, slot, 2))

            def cross_exps():
                for b in range(BATCH):
                    act.wait_ge(xmax_done, b + 1)
                    for m in range(2):
                        last = act.activation(energy[:, b, m, :], proj_bank[b][:, m * SEQ:(m + 1) * SEQ], ACT.Exp,
                                              bias=xmax[:, b, m:m + 1], accum_out=xsum[:, b, m:m + 1])
                    last.then_inc(xexp_done, 1)

            def copy_mix():
                for b in range(BATCH):
                    act.wait_ge(mix_ready, b + 1)
                    act.activation(mix_T[:, b, :, :].rearrange("p k n -> p (k n)"), proj_bank[b][:, :],
                                   ACT.Copy).then_inc(mix_copied, 1)

            def add_bias(n):
                act.wait_ge(xproj_ready, n + 1)
                act.wait_ge(ctx_in[0], 32)
                dst, o = (xq_sb, xk_sb)[n % 2], (n // 2) * PAIR
                act.activation(dst[:, o:o + PAIR], proj_bank[n][:, :], ACT.Identity,
                               bias=xbias[:, n % 2:n % 2 + 1]).then_inc(xproj_copied, 1)


            shifts = 0

            def norm_apply(norm, part, done):
                nonlocal shifts
                shifts += part[1]
                act.wait_ge(shift_done, shifts)
                for m in range(part[0], end(part)):
                    src = bank_y[m][:, 0:DM] if residual_in_bank(norm, part) else acc[:, m, :]
                    act.activation(acc[:, m, :], src, ACT.Identity, bias=nshift[:, norm, m:m + 1],
                                   scale=rstd[:, norm, m:m + 1]).then_inc(done, 1)

            def copy_T(src, dst, part, copied):
                n = part[1] * P
                act.activation(dst, src[:, 0:KT * n].rearrange("p (k n) -> p k n", k=KT),
                               ACT.Copy).then_inc(copied, part[1])

            def copy_x1T(part):
                act.wait_ge(x1T_ready, end(part))
                copy_T(bank_x1T[part[0]], x1_T(part), part, x1T_copied)

            def copy_x2T(part):
                act.wait_ge(x2T_ready, end(part))
                copy_T(bank_x2T[part[0]], x2_T(part), part, x2T_copied)

            def copy_ff(part):
                o = DM if residual_in_bank(2, part) else 0
                for m in range(part[1]):
                    act.wait_ge(ff_ready, part[0] + m + 1)
                    act.activation(ff(part)[:, m, o:FW], bank_ff[part[0]][m][:, o:FW],
                                   ACT.Copy).then_inc(ff_copied, 1)

            def gate_exps(part):
                act.wait_ge(lmax_done, end(part))
                for m in range(part[1]):
                    i = part[0] + m
                    act.activation(lexp[:, i, :], ff(part)[:, m, DM:DM + EXPERTS], ACT.Exp,
                                   bias=nlmax[:, i:i + 1]).then_inc(lexp_done, 1)

            def copy_loraT(part):
                act.wait_ge(lT_ready, end(part))
                act.activation(lora_tT(part), bank_lT[part[0]][:, 0:part[1] * P],
                               ACT.Copy, scale=LORA_ALPHA).then_inc(lT_copied, part[1])

            add_bias(0)
            weight_high(QK_H0, 0, 0)
            for n in (1, 2, 3):
                add_bias(n)
            act.wait_ge(zeroed, 3)
            all_steps(act, step)

            copy_probs(LAST_IT, 2)
            copy_values(LAST_IT, 3)
            exps(LAST_IT, 3)
            head_high(LAST_IT, 2)
            copy_probs(LAST_IT, 3)
            head_high(LAST_IT, 3)
            copy_x2T(B1)
            copy_ff(B1)
            copy_x1T(T4)
            copy_x1T(T5)
            gate_exps(B1)
            copy_x1T(T6)
            copy_x1T(T7)
            copy_loraT(B1)
            copy_x2T(T4)
            copy_x2T(T5)
            copy_ff(T4)
            copy_ff(T5)
            copy_x2T(T6)
            copy_x2T(T7)
            gate_exps(T45)
            copy_ff(T6)
            copy_ff(T7)
            norm_apply(2, B1, x3_done_act)
            copy_loraT(T4)
            copy_loraT(T5)
            gate_exps(T67)
            copy_loraT(T6)
            copy_loraT(T7)
            norm_apply(2, T4, x3_done_act)
            norm_apply(2, T5, x3_done_act)

        @block.gpsimd
        def _(pool):
            def weight_low(piece, it, slot):
                wait_piece(pool, hi_done[piece], it, slot)
                pool.tensor_tensor(weight_part(piece, it, slot, 1), staged(piece),
                                   weight_part(piece, it, slot, 0).bitcast(F32),
                                   ALU.subtract).then_inc(lo_done[piece], 1)

            def rotate(it, slot, scaled, n, dst, rotated):
                wait(pool, scaled, it, slot, 1, 1)
                wait(pool, scores_ready, it, slot, 2, -2)
                pool.tensor_tensor(dst[:, slot % 2, :], rope[:, n, :], rope[:, n + 1, :],
                                   ALU.add).then_inc(rotated, 1)

            def step(it, slot):
                if present(it, slot, -1):
                    ahead = back(it, slot, -1)
                    weight_low(ahead[1] % 2, *ahead)
                if half_of(it) == 0:
                    weight_low((WV, WO)[slot % 2], it, slot)
                rotate(it, slot, q_scaled, 0, qr, q_rotated)
                rotate(it, slot, k_scaled, 2, kr, k_rotated)
                if first(it) and slot == 2:
                    pool.wait_ge(xhi_done, 2)
                    pool.tensor_tensor(x_lo[:, :, PAIR:2 * PAIR], x_second,
                                       x_hi[:, :, PAIR:2 * PAIR].bitcast(F32), ALU.subtract).then_inc(x_split, 1)
                if last(it, slot, 0):
                    inverse_std(0, B0)
                    inverse_std(0, B1)
                if last(it, slot, 1):
                    inverse_std(1, B0)
                if last(it, slot, 2):
                    add_dense(B0)
                if last(it, slot, 3):
                    inverse_std(2, B0)

            count = 0

            def inverse_std(norm, part):
                nonlocal count
                i, z = part[0], end(part)
                pool.wait_ge(ln_moments[norm], z)
                pool.tensor_scalar(veps[:, norm, i:z], moments[:, norm, i:z, 1], EPS, None,
                                   ALU.add).then_inc(ln_veps, 1)
                count += 1
                pool.wait_ge(ln_veps, count)
                pool.tensor_tensor(rstd[:, norm, i:z], veps[:, norm, i:z], power[:, 0:z - i],
                                   ALU.pow).then_inc(ln_rstd[norm], z - i)

            def shift(norm, part):
                pool.wait_ge(ln_rstd[norm], end(part))
                for m in range(part[0], end(part)):
                    pool.tensor_scalar(nshift[:, norm, m:m + 1], moments[:, norm, m, 0:1], rstd[:, norm, m:m + 1],
                                       -1.0, ALU.mult, ALU.mult).then_inc(shift_done, 1)

            def add_dense(part):
                pool.wait_ge(ff_copied, end(part))
                pool.tensor_tensor(rows(part), rows(part), ff(part)[:, :, 0:DM],
                                   ALU.add).then_inc(base_done, part[1])

            pool.wait_ge(zeroed, 3)
            weight_low(QK_H0, 0, 0)
            all_steps(pool, step)

            inverse_std(1, B1)
            inverse_std(0, T4)
            inverse_std(0, T5)
            inverse_std(0, T6)
            inverse_std(0, T7)
            add_dense(B1)
            for part in (T4, T5, T6, T7):
                inverse_std(1, part)
            inverse_std(2, B1)
            shift(2, B1)
            inverse_std(2, T45)
            shift(2, T45)
            inverse_std(2, T6)
            inverse_std(2, T7)


def kernel(**inputs):
    import numpy as np
    import concourse.bacc as bacc
    from concourse.bass_utils import run_bass_kernel_spmd

    f32 = np.float32
    a = {k: np.asarray(v) for k, v in inputs.items()}
    x = a["x"].reshape(TOK, DM)
    wqkv, inner = a["L0_attn_w_qkv"], HEADS * HD

    qk = wqkv[:2 * inner].reshape(2, GROUPS, 2, HD, KT, P)
    v = wqkv[2 * inner:].reshape(GROUPS, 2 * HD, KT, P)
    o = a["L0_attn_w_o"].reshape(DM, GROUPS, 2, HD)
    lay = {
        "x_nat": x.reshape(TILES, P, DM).transpose(1, 0, 2),
        "x_T": x.reshape(TOK, KT, P).transpose(2, 1, 0),
        "ctx_T": a["ctx_1024"].reshape(TOK, CTX).T,
        "w_qk": qk.transpose(1, 5, 2, 0, 4, 3).reshape(GROUPS, P, 2 * PIECE),
        "w_v": v.transpose(0, 3, 2, 1).reshape(GROUPS, P, PIECE),
        "w_o": o.transpose(1, 3, 2, 0).reshape(GROUPS, P, PIECE),
        "cross_wT": np.concatenate([a["L0_xattn_Wq"].T, a["L0_xattn_Wk"].T,
                                    np.stack([a["L0_xattn_bq"], a["L0_xattn_bk"]], axis=1)], axis=1),
        "ffn_T": np.concatenate([a["L0_ffn_weight"], a["L0_ffn_gate_w"],
                                 a["L0_ffn_A_w"].reshape(EXPERTS * RANK, DM)], axis=0)
                   .reshape(FW, KT, P).transpose(2, 1, 0),
        "lora_bT": a["L0_ffn_B_w"].transpose(0, 2, 1).reshape(EXPERTS * RANK, DM),
    }

    half = HD // 2
    inv_freq = (f32(1.0) / f32(10000.0) ** (np.arange(0, HD, 2, dtype=f32) / f32(HD))).astype(f32)
    angle = inv_freq[:, None] * np.arange(SEQ, dtype=f32)[None, :]
    cos, sin = np.cos(angle).astype(f32), np.sin(angle).astype(f32)
    query = np.arange(P)[:, None]
    key0, key1 = np.arange(S0)[None, :], np.arange(WINDOW, SEQ)[None, :]
    seen = np.concatenate([(key0 <= query) & (key0 > query - WINDOW),
                           (key1 <= query + P) & (key1 > query + P - WINDOW)], axis=1)
    expert = np.arange(EXPERTS)
    lay |= {
        "rope_cos": np.tile(np.concatenate([cos, cos]), (1, 2)),
        "rope_sin": np.tile(np.concatenate([sin, -sin]), (1, 2)),
        "score_mask": np.where(seen, f32(0), f32(-1e30)),
        "identity": np.eye(P, dtype=f32),
        "below": np.tile((expert[None, :] < expert[:, None]).astype(f32).reshape(1, -1), (P, 1)),
    }

    nc = bacc.Bacc("TRN2", target_bir_lowering=False, num_devices=1)
    arrays, args = {}, []
    for name, value in lay.items():
        arrays[name + "_dram"] = np.ascontiguousarray(value)
        args.append(nc.dram_tensor(name + "_dram", value.shape, F32, kind="ExternalInput").ap())
    args.append(nc.dram_tensor("out_dram", (P, TILES, DM), F32, kind="ExternalOutput").ap())
    build(nc, *args)
    r = run_bass_kernel_spmd(nc, [arrays], core_ids=[0])
    got = r.results[0]["out_dram"]
    return np.ascontiguousarray(got.transpose(1, 0, 2)).reshape(BATCH, SEQ, DM)
```
